# Optimizing a Trainium2 kernel written in Bass

```python
import numpy as np
import jax
import jax.numpy as jnp

def _softmax(x, axis=-1):
    return jax.nn.softmax(x, axis=axis)

def _gelu(x):
    return jax.nn.gelu(x, approximate=True)

def _silu(x):
    return jax.nn.silu(x)

def _sigmoid(x):
    return jax.nn.sigmoid(x)

def _layernorm(x, axis=-1, eps=1e-05):
    m = jnp.mean(x, axis=axis, keepdims=True)
    v = jnp.var(x, axis=axis, keepdims=True)
    return (x - m) / jnp.sqrt(v + eps)

def _scatter_add(tgt, idx, src, axis=0):
    return tgt.at[idx].add(src)

def _segment_sum(src, seg, n):
    return jax.ops.segment_sum(src, seg, n)
kernel_name = 'mk_lm_tower_d1_tok_ids2048_r4_fe0bb3'

def setup_inputs(seed: int=0):
    np.random.seed(seed)
    _w = jnp.asarray

    def _rec_inputs():
        import jax
        import jax.numpy as jnp
        _rk = jax.random.key(seed)
        x = jax.random.randint(jax.random.fold_in(_rk, 1), (2, 1024), 0, 127998, jnp.int32)
        return x
    x = _rec_inputs()

    def _L0_tok_setup():
        import jax, jax.numpy as jnp
        import numpy as np
        VOCAB = 32000
        D_MODEL = 512
        LATENT = 128
        NUM_HOT = 8000

        def _maps(hot_token_ids, vocab):
            hot_mask = jnp.zeros((vocab,), dtype=bool).at[hot_token_ids].set(True)
            tok2hot = jnp.full((vocab,), 0, dtype=jnp.int32).at[hot_token_ids].set(jnp.arange(hot_token_ids.shape[0], dtype=jnp.int32))
            tok2cold = jnp.cumsum((~hot_mask).astype(jnp.int32)) - 1
            tok2cold = jnp.clip(tok2cold, 0, None)
            return (hot_mask, tok2hot, tok2cold)
        key = jax.random.key(seed)
        k1, k2, k3, k4 = jax.random.split(key, 4)
        input_ids = jax.random.randint(k1, (4, 1024), 0, VOCAB, dtype=jnp.int64 if jax.config.jax_enable_x64 else jnp.int32)
        hot_token_ids = jnp.arange(NUM_HOT, dtype=jnp.int32)
        hot_emb_w = jax.random.normal(k2, (NUM_HOT, D_MODEL), dtype=jnp.float32)
        cold_emb_w = jax.random.normal(k3, (VOCAB - NUM_HOT, LATENT), dtype=jnp.float32)
        proj_w = jax.random.normal(k4, (D_MODEL, LATENT), dtype=jnp.float32) / np.sqrt(LATENT)
        return {'input_ids': input_ids, 'hot_token_ids': hot_token_ids, 'hot_emb_w': hot_emb_w, 'cold_emb_w': cold_emb_w, 'proj_w': proj_w}
    _L0_tok_all = _L0_tok_setup()
    _L0_tok_in = {k: v for k, v in _L0_tok_all.items() if k in ('hot_token_ids', 'hot_emb_w', 'cold_emb_w', 'proj_w')}
    del _L0_tok_all

    def _L0_attn_setup():
        import jax, jax.numpy as jnp
        import numpy as np
        import math
        D_MODEL = 512
        NUM_HEAD = 16
        HEAD_DIM = D_MODEL // NUM_HEAD

        def _trunc_normal(key, shape, std):
            return jax.random.truncated_normal(key, -3.0, 3.0, shape, dtype=jnp.float32) * std
        key = jax.random.key(seed)
        kx, kp, ko = jax.random.split(key, 3)
        b, s = (4, 512)
        x = jax.random.normal(kx, (b, s, D_MODEL), dtype=jnp.float32)
        sigma_p = math.sqrt(2.0 / (D_MODEL + 3 * D_MODEL))
        w_project = _trunc_normal(kp, (3 * D_MODEL, D_MODEL), sigma_p)
        sigma_o = math.sqrt(2.0 / (D_MODEL + D_MODEL))
        w_out = _trunc_normal(ko, (D_MODEL, D_MODEL), sigma_o)
        return {'x': x, 'w_project': w_project, 'w_out': w_out}
    _L0_attn_all = _L0_attn_setup()
    _L0_attn_in = {k: v for k, v in _L0_attn_all.items() if k in ('w_project', 'w_out')}
    del _L0_attn_all

    def _L0_ffn_setup():
        import jax, jax.numpy as jnp
        import numpy as np
        TOPK = 2
        NORM_TOPK = True
        SCALE = 1.0
        EPS = 1e-09
        key = jax.random.key(seed)
        ks = jax.random.split(key, 9)
        h, i, E = (512, 256, 16)
        std = 0.02
        return {'x': jax.random.normal(ks[0], (1, 512, h), jnp.float32), 'Wr': jax.random.normal(ks[1], (E, h), jnp.float32) * std, 'bias': jnp.zeros((E,), jnp.float32), 'Wg': jax.random.normal(ks[2], (E, h, i), jnp.float32) * std, 'Wu': jax.random.normal(ks[3], (E, h, i), jnp.float32) * std, 'Wd': jax.random.normal(ks[4], (E, i, h), jnp.float32) * std, 'sWg': jax.random.normal(ks[5], (h, i), jnp.float32) * std, 'sWu': jax.random.normal(ks[6], (h, i), jnp.float32) * std, 'sWd': jax.random.normal(ks[7], (i, h), jnp.float32) * std}
    _L0_ffn_all = _L0_ffn_setup()
    _L0_ffn_in = {k: v for k, v in _L0_ffn_all.items() if k in ('Wr', 'bias', 'Wg', 'Wu', 'Wd', 'sWg', 'sWu', 'sWd')}
    del _L0_ffn_all
    return {'x': x, 'L0_tok_hot_token_ids': _L0_tok_in['hot_token_ids'], 'L0_tok_hot_emb_w': _L0_tok_in['hot_emb_w'], 'L0_tok_cold_emb_w': _L0_tok_in['cold_emb_w'], 'L0_tok_proj_w': _L0_tok_in['proj_w'], 'L0_attn_w_project': _L0_attn_in['w_project'], 'L0_attn_w_out': _L0_attn_in['w_out'], 'L0_ffn_Wr': _L0_ffn_in['Wr'], 'L0_ffn_bias': _L0_ffn_in['bias'], 'L0_ffn_Wg': _L0_ffn_in['Wg'], 'L0_ffn_Wu': _L0_ffn_in['Wu'], 'L0_ffn_Wd': _L0_ffn_in['Wd'], 'L0_ffn_sWg': _L0_ffn_in['sWg'], 'L0_ffn_sWu': _L0_ffn_in['sWu'], 'L0_ffn_sWd': _L0_ffn_in['sWd']}

def reference(x, L0_tok_hot_token_ids, L0_tok_hot_emb_w, L0_tok_cold_emb_w, L0_tok_proj_w, L0_attn_w_project, L0_attn_w_out, L0_ffn_Wr, L0_ffn_bias, L0_ffn_Wg, L0_ffn_Wu, L0_ffn_Wd, L0_ffn_sWg, L0_ffn_sWu, L0_ffn_sWd):
    import jax
    import jax.numpy as jnp

    def _L0_tok_ref(input_ids, hot_token_ids, hot_emb_w, cold_emb_w, proj_w):
        import jax, jax.numpy as jnp
        import numpy as np
        VOCAB = 32000
        D_MODEL = 512
        LATENT = 128
        NUM_HOT = 8000

        def _maps(hot_token_ids, vocab):
            hot_mask = jnp.zeros((vocab,), dtype=bool).at[hot_token_ids].set(True)
            tok2hot = jnp.full((vocab,), 0, dtype=jnp.int32).at[hot_token_ids].set(jnp.arange(hot_token_ids.shape[0], dtype=jnp.int32))
            tok2cold = jnp.cumsum((~hot_mask).astype(jnp.int32)) - 1
            tok2cold = jnp.clip(tok2cold, 0, None)
            return (hot_mask, tok2hot, tok2cold)
        hot_mask, tok2hot, tok2cold = _maps(hot_token_ids, VOCAB)
        flat = input_ids.reshape(-1)
        is_hot = hot_mask[flat]
        hot_vec = hot_emb_w[tok2hot[flat]]
        cold_lat = cold_emb_w[tok2cold[flat]]
        cold_vec = cold_lat @ proj_w.T
        out = jnp.where(is_hot[:, None], hot_vec, cold_vec)
        return out.reshape(*input_ids.shape, D_MODEL)

    def _L0_attn_ref(x, w_project, w_out):
        import jax, jax.numpy as jnp
        import numpy as np
        import math
        D_MODEL = 512
        NUM_HEAD = 16
        HEAD_DIM = D_MODEL // NUM_HEAD

        def _trunc_normal(key, shape, std):
            return jax.random.truncated_normal(key, -3.0, 3.0, shape, dtype=jnp.float32) * std
        b, s, d = x.shape
        qkv = jnp.einsum('bsd,od->bso', x, w_project)
        qkv = qkv.reshape(b, s, 3, NUM_HEAD, HEAD_DIM)
        qkv = jnp.transpose(qkv, (2, 0, 3, 1, 4))
        q, k, v = (qkv[0], qkv[1], qkv[2])
        att = jnp.einsum('bhqd,bhkd->bhqk', q, k) / math.sqrt(HEAD_DIM)
        causal = jnp.triu(jnp.ones((s, s), dtype=bool), k=1)
        att = jnp.where(causal[None, None, :, :], jnp.float32(-1000000000.0), att)
        att = jax.nn.softmax(att, axis=-1)
        out = jnp.einsum('bhqk,bhkd->bhqd', att, v)
        out = jnp.transpose(out, (0, 2, 1, 3)).reshape(b, s, d)
        return jnp.einsum('bsd,od->bso', out, w_out)

    def _L0_ffn_ref(x, Wr, bias, Wg, Wu, Wd, sWg, sWu, sWd):
        import jax, jax.numpy as jnp
        import numpy as np
        TOPK = 2
        NORM_TOPK = True
        SCALE = 1.0
        EPS = 1e-09
        b, s, h = x.shape
        E = Wr.shape[0]
        xt = x.reshape(b * s, h)
        logits = xt @ Wr.T + bias
        probs = jax.nn.softmax(logits, axis=-1)
        topk_val, topk_idx = jax.lax.top_k(probs, TOPK)
        if NORM_TOPK:
            w = topk_val / (jnp.sum(topk_val, axis=-1, keepdims=True) + EPS)
        else:
            w = topk_val
        w = w * SCALE
        g = jnp.einsum('th,ehi->tei', xt, Wg)
        u = jnp.einsum('th,ehi->tei', xt, Wu)
        y = jnp.einsum('tei,eih->teh', jax.nn.silu(g) * u, Wd)
        oh = jax.nn.one_hot(topk_idx, E, dtype=x.dtype)
        routed = jnp.einsum('tke,tk,teh->th', oh, w, y)
        shared = jax.nn.silu(xt @ sWg) * (xt @ sWu) @ sWd
        return (routed + shared).reshape(b, s, h)
    h = _L0_tok_ref(x, L0_tok_hot_token_ids, L0_tok_hot_emb_w, L0_tok_cold_emb_w, L0_tok_proj_w)
    h = h + _L0_attn_ref(_layernorm(h, axis=-1), L0_attn_w_project, L0_attn_w_out)
    h = h + _L0_ffn_ref(_layernorm(h, axis=-1), L0_ffn_Wr, L0_ffn_bias, L0_ffn_Wg, L0_ffn_Wu, L0_ffn_Wd, L0_ffn_sWg, L0_ffn_sWu, L0_ffn_sWd)
    return h

_drawn_inputs = setup_inputs


def setup_inputs(seed=0):
    import zlib

    import numpy as np

    out = dict(_drawn_inputs(seed))
    spreads = {'L0_ffn_bias': (0.0, 2.0)}
    factors = {'L0_ffn_Wr': 10.629}
    for name, (base, spread) in spreads.items():
        noise = np.random.default_rng([zlib.crc32(name.encode()), seed]).standard_normal(out[name].shape)
        drawn = base * np.exp(spread * noise) if base else spread * noise
        out[name] = jnp.asarray(drawn.astype(out[name].dtype))
    for name, factor in factors.items():
        out[name] = (out[name] * factor).astype(out[name].dtype)
    return out
```

```python
from contextlib import ExitStack

import concourse.bass as bass
from concourse import mybir

F32 = mybir.dt.float32
F32R = mybir.dt.float32r
BF16 = mybir.dt.bfloat16
I32 = mybir.dt.int32
U32 = mybir.dt.uint32
ALU = mybir.AluOpType
ACT = mybir.ActivationFunctionType
AX = mybir.AxisListType

P = 128
VOCAB, NUM_HOT, NUM_COLD = 32000, 8000, 24000
BATCH, SEQ, D = 2, 1024, 512
T = BATCH * SEQ
NT = T // P
KC = D // P
LATENT = 128
HEADS, HD = 16, 32
GROUPS, GH = HEADS // 4, 4
ATT_SCALE = float(HD) ** -0.5
QT = SEQ // P
LN_EPS = 1e-5
E, TOPK, FF = 16, 2, 256
W_EPS = 1e-9
HI = VOCAB // 256
HOT_P, HOT_C = 125, 64
SKIP = 100000.0
TILES = TOPK * T // P + E
RING = 8
WRING = 4
LAG = 4
PSLOTS = 2


class Chain:

    def __init__(self, eng, sem, start=0):
        self.eng, self.sem, self.n = eng, sem, start

    def __call__(self, ins):
        ins.then_inc(self.sem, 1)
        self.n = self.n + 1
        self.eng.wait_ge(self.sem, self.n)


def build(nc, a, out):
    ctx = ExitStack()
    with ctx:
        def sb(name, shape, dt=F32, where=ctx):
            return where.enter_context(nc.sbuf_tensor(name, shape, dt))

        def sem(name):
            return ctx.enter_context(nc.semaphore(name))

        ident = sb("ident", [P, P])
        ident_bf = sb("ident_bf", [P, P], BF16)
        tri_bf = sb("tri_bf", [P, P], BF16)
        ones_bf = sb("ones_bf", [P, P], BF16)
        mask_bf = sb("mask_bf", [P, P], BF16)
        iota_bf = sb("iota_bf", [P, 256], BF16)
        half_neg = sb("half_neg", [P, 1])
        iota_e = sb("iota_e", [P, E])
        iota_p128 = sb("iota_p128", [P, T // P])
        iota_j = sb("iota_j", [P, TILES])
        iota_f = sb("iota_f", [P, P])
        tok_no1 = sb("tok_no1", [P, NT])
        upto_e = sb("upto_e", [P, E, E])

        psum = ctx.enter_context(nc.psum_tensor("psum", [P, 8, 512], F32))

        def bank(i, n=1):
            return psum[:, i:i + n, :].rearrange("p a n -> p (a n)")

        xn2_dram = nc.dram_tensor("xn2_scratch", [T, D], F32, kind="Internal").ap()
        h_dram = nc.dram_tensor("h_scratch", [T, D], F32, kind="Internal").ap()

        xnT = sb("xnT", [P, KC, T])

        tok_ctx = ExitStack()
        tk = lambda name, shape, dt=F32: sb(name, shape, dt, tok_ctx)
        hot_ids = tk("hot_ids", [HOT_P, HOT_C], I32)
        tok_ids = tk("tok_ids", [P, NT], I32)
        hot_f = tk("hot_f", [HOT_P, HOT_C])
        hot_wrap = tk("hot_wrap", [HOT_P, HOT_C])
        hot_hi = tk("hot_hi", [HOT_P, HOT_C])
        hot_lo = tk("hot_lo", [HOT_P, HOT_C])
        hot_i = tk("hot_i", [HOT_P, 2, HOT_C], I32)
        row64 = tk("row64", [HOT_P, 1])
        chunk1 = tk("chunk1", [HOT_P, HOT_C])
        tok_f = tk("tok_f", [P, NT])
        tok_wrap = tk("tok_wrap", [P, NT])
        tok_i = tk("tok_i", [P, 3, NT], I32)
        tok_hi = tk("tok_hi", [P, NT])
        tok_lo = tk("tok_lo", [P, NT])
        oh_hi = tk("oh_hi", [HOT_P, HOT_C, HI], BF16)
        oh_hi_row = tk("oh_hi_row", [HOT_P, HOT_C, HI], BF16)
        oh_lo = tk("oh_lo", [HOT_P, HOT_C, 2, 256], BF16)
        seen = tk("seen", [HI, 256])
        seen_n = tk("seen_n", [HI, 1])
        seen_b = tk("seen_b", [HI, 1], BF16)
        rank_i = tk("rank_i", [HI, 3, 256], I32)
        tab_a = tk("tab_a", [HI, 512], BF16)
        tab_b = tk("tab_b", [HI, 256], BF16)
        tab_c = tk("tab_c", [HI, 1], BF16)
        tok_oh = tk("tok_oh", [P, NT, HI], BF16)
        tok_ohT = tk("tok_ohT", [HI, NT, P], BF16)
        pick = tk("pick", [P, 2, 2, 256], BF16)
        prod = tk("prod", [P, 2, 2, 256])
        below = tk("below", [P, NT])
        hot_no = tk("hot_no", [P, NT])
        tmp_a = tk("tmp_a", [P, NT])
        tmp_b = tk("tmp_b", [P, NT])
        hot_row = tk("hot_row", [P, NT], I32)
        cold_row = tk("cold_row", [P, NT], I32)
        projT = tk("projT", [LATENT, D])
        hot_vec = [tk(f"hot_vec{i}", [P, D]) for i in range(RING)]
        cold_lat = [tk(f"cold_lat{i}", [P, LATENT]) for i in range(RING)]
        cold_T = tk("cold_T", [P, 2, P])
        stats = tk("stats", [P, 2, 6])
        mv = tk("mv", [P, 2, 2])
        rstd = tk("rstd", [P, 2])
        xn = tk("xn", [P, 2, D])
        tok_ctx.close()

        attnT = sb("attnT", [P, GROUPS * T])
        att_ctx = ExitStack()
        ak = lambda name, shape, dt=F32: sb(name, shape, dt, att_ctx)
        w_unit = ak("w_unit", [P, KC, 3 * P])
        q_stack = [ak(f"q_stack{b}", [P, GH, SEQ], F32R) for b in range(BATCH)]
        k_stack = [ak(f"k_stack{b}", [P, GH, SEQ], F32R) for b in range(BATCH)]
        v_unit = [ak(f"v_unit{b}", [P, QT, P]) for b in range(BATCH)]
        full = ak("full", [P, 2, 512])
        part_hi = ak("part_hi", [P, 2, SEQ], F32R)
        part_lo = ak("part_lo", [P, 2, SEQ], F32R)
        nmax = ak("nmax", [P, 4])
        probs = [ak(f"probs{i}", [P, SEQ]) for i in range(PSLOTS)]
        probsT = [ak("probsT0", [P, GH, SEQ - P]), ak("probsT1", [P, GH, SEQ])]
        z_sum = ak("z_sum", [P, 2, GH])
        z_rec = ak("z_rec", [P, 2, GH])
        z_inv = ak("z_inv", [P, 2, GH, HD])
        z_rows = ak("z_rows", [P, 2, P])
        att_ctx.close()

        acc = sb("acc", [P, NT, D])
        wo = sb("wo", [P, KC, D])
        wr = sb("wr", [P, KC, E])
        bias = sb("bias", [P, E])
        xn2 = sb("xn2", [P, 2, D])
        stats2 = sb("stats2", [P, 2, 6])
        mv2 = sb("mv2", [P, 2, 2])
        rstd2 = sb("rstd2", [P, 2])
        w_sgu = sb("w_sgu", [P, KC, D])
        w_sd = sb("w_sd", [P, 2, D])
        w_dn = sb("w_dn", [P, WRING, 2, D])
        logits = sb("logits", [P, NT, E])
        row_red = sb("row_red", [P, NT])
        probs_e = sb("probs_e", [P, NT, E])
        top_v = sb("top_v", [P, NT, 8])
        top_i = sb("top_i", [P, NT, 8], U32)
        top_f = sb("top_f", [P, NT, TOPK])
        w_sum = sb("w_sum", [P, NT])
        w_top = sb("w_top", [P, NT, TOPK])
        oh_e = sb("oh_e", [P, TOPK, NT, E])
        oh_any = sb("oh_any", [P, NT, E], BF16)
        count_e = sb("count_e", [P, E])
        cmp_e = sb("cmp_e", [P, E, E])
        tiles_e = sb("tiles_e", [P, E])
        tiles_to = sb("tiles_to", [P, E])
        tiles_to_i = sb("tiles_to_i", [P, E], I32)
        base_e = sb("base_e", [P, E])
        pos_all = sb("pos_all", [P, NT, E])
        pos_pick = sb("pos_pick", [P, NT, E])
        pos_f = sb("pos_f", [P, TOPK, NT])
        pos_i = sb("pos_i", [P, TOPK, NT], I32)
        pos_hl = sb("pos_hl", [P, 2, TOPK, NT], I32)
        pos_hlf = sb("pos_hlf", [P, 2, TOPK, NT])
        cmp_j = sb("cmp_j", [P, TILES, E])
        tile_e = sb("tile_e", [P, TILES])
        tile_e_i = sb("tile_e_i", [P, TILES], I32)
        slot_lo = sb("slot_lo", [P, 4, P])
        slot_hi = sb("slot_hi", [P, 4, 2, TILES])
        slot_f = sb("slot_f", [P, TILES])
        slot_tok = sb("slot_tok", [P, TILES], I32)
        slot_w = sb("slot_w", [P, TILES])
        slot_pad = sb("slot_pad", [P, TILES])
        slot_out = sb("slot_out", [P, TILES], I32)
        pad_row = sb("pad_row", [P, 1])
        out_no = [sb(f"out_no{i}", [P, 1], I32) for i in range(2)]
        rows_no = [sb(f"rows_no{i}", [P, 1], I32) for i in range(2)]
        x_rows = [sb(f"x_rows{i}", [P, D]) for i in range(2)]
        x_T = sb("x_T", [P, 2, D])
        silu_g = sb("silu_g", [P, 2, FF])
        gated = sb("gated", [P, 2, FF])
        gated_T = sb("gated_T", [P, 2, FF])
        y_sb = sb("y_sb", [P, 2, D])

        w_gu = attnT[:, :].rearrange("p (s k n) -> p s k n", s=WRING, k=KC)

        s_dve2 = sem("dve_router_step")
        s_passed = sem("pool_waits_passed")
        s_moec = sem("router_constants_ready")
        s_wo = sem("output_weights_loaded")
        s_rtw = sem("router_weights_loaded")
        s_hl = [sem(f"h_loaded{i}") for i in range(NT)]
        s_sw = sem("shared_weights_loaded")
        s_op = sem("output_projected")
        s_acc = sem("residual_ready")
        s_var2 = sem("variance2_ready")
        s_rstd2 = sem("rstd2_ready")
        s_xn2 = sem("xn2_ready")
        s_xst = [sem(f"xn2_stored{i}") for i in range(2)]
        s_x2T = sem("xn2_turned")
        s_x2C = sem("xn2T_ready")
        s_lg = sem("logits_summed")
        s_lgc = sem("logits_copied")
        s_shift = sem("logits_shifted")
        s_exp = sem("router_exp_ready")
        s_oh = sem("choices_ready")
        s_rank = sem("ranks_summed")
        s_slot = sem("slot_onehots_ready")
        s_slotm = sem("slot_matmuls_done")
        s_plan = sem("plan_ready")
        s_gu = sem("gate_up_ready")
        s_silu = sem("silu_ready")
        s_gated = sem("gated_ready")
        s_gT = sem("gated_turned")
        s_gC = sem("gated_T_ready")
        s_y = sem("down_ready")
        s_yc = sem("y_copied")
        s_rn = sem("row_numbers_copied")
        s_xg = [sem(f"rows_gathered{i}") for i in range(2)]
        s_xT2 = sem("rows_turned")
        s_xC2 = sem("rows_T_ready")
        s_wl = [sem(f"expert_loaded{i}") for i in range(WRING)]
        s_wr = sem("expert_weights_ready")
        s_on = sem("out_row_numbers_copied")
        s_yadd = sem("y_added")
        s_pad = sem("spare_rows_stored")
        s_out = [sem(f"out_stored{i}") for i in range(NT)]
        s_w = sem("unit_weights_loaded")
        s_fill = sem("projection_ready")
        s_fact = sem("projection_copied_by_act")
        s_fdve = sem("projection_copied_by_dve")
        s_hi = sem("high_parts_ready")
        s_lo = sem("low_parts_ready")
        s_stack = [sem(f"stacks_loaded{b}") for b in range(BATCH)]
        s_S = sem("scores_ready")
        s_M = sem("row_max_ready")
        s_E = sem("probs_ready")
        s_T = sem("probs_turned")
        s_Ca = sem("probsT_copied_by_act")
        s_Cd = sem("probsT_copied_by_dve")
        s_Zr = sem("z_reciprocal_ready")
        s_Z = sem("z_inverse_ready")
        s_PV = sem("heads_summed")
        s_ZR = sem("z_rows_ready")
        s_AT = sem("attnT_ready")
        s_in = sem("ids_loaded")
        s_proj = sem("projT_loaded")
        s_const = sem("constants_ready")
        s_pool = sem("pool_step")
        s_dve = sem("dve_step")
        s_act = sem("act_step")
        s_ohhi = sem("hot_onehot_hi_ready")
        s_ohlo = sem("hot_onehot_lo_ready")
        s_row = sem("hot_row_part_ready")
        s_chunk = sem("hot_chunk_part_ready")
        s_table = sem("table_summed")
        s_seen = sem("seen_counted")
        s_base = sem("base_summed")
        s_tab = sem("tables_ready")
        s_toh = sem("token_onehot_ready")
        s_tohT = sem("token_onehot_turned")
        s_tohC = sem("token_onehot_copied")
        s_look = sem("lookup_multiplied")
        s_looked = sem("lookup_reduced")
        s_rows = sem("row_numbers_ready")
        s_hotg = [sem(f"hot_gathered{i}") for i in range(RING)]
        s_coldg = [sem(f"cold_gathered{i}") for i in range(RING)]
        s_coldT = sem("cold_turned")
        s_coldC = sem("cold_copied")
        s_cvec = sem("cold_projected")
        s_h = sem("h_ready")
        s_hst = [sem(f"h_stored{i}") for i in range(RING)]
        s_var = sem("variance_ready")
        s_rstd = sem("rstd_ready")
        s_xn = sem("xn_ready")
        s_xT = sem("xn_turned")
        s_xC = sem("xnT_ready")
        block = ctx.enter_context(nc.Block())

        BATCHES = 4
        PER = NT // BATCHES

        HEAD = 16
        STACKED = 16 * 8 * GH
        STEPS = QT * GH
        FILLS = 6

        def turned_banks(i):
            return 1 if i < 4 else 2

        def copier(i, h, k):
            if i >= 4:
                return "act" if k == 0 else "dve"
            return "dve" if h % 2 == 0 else "act"

        banks = [(i, h, k) for i in range(QT) for h in range(GH) for k in range(turned_banks(i))]
        UB = len(banks)
        UCOPY = {e: sum(copier(*x) == e for x in banks) for e in ("act", "dve")}

        def bank_no(i, h, k):
            return banks.index((i, h, k))

        def copies(e, upto):
            return sum(copier(*x) == e for x in banks[:upto])

        def wait_bank_free(pe, u, n):
            m = n - 2
            x = banks[m % UB]
            v = u if m >= 0 else u - 1
            e = copier(*x)
            pe.wait_ge(s_Ca if e == "act" else s_Cd, HEAD + v * UCOPY[e] + copies(e, m % UB + 1))

        def att_sp(sp):
            def load_w(g):
                sp.dma_start(w_unit[:, :, :], a["wqkv"][g] if isinstance(g, int) else
                             a["wqkv"][bass.ds(g, 1), :, :, :].rearrange("o p k n -> (o p) k n")).then_inc(s_w, 16)

            def stack(u, b, first=False):
                if not first:
                    sp.wait_ge(s_S, HEAD + (u - 1) * STEPS)
                for side, st in ((0, q_stack[b]), (1, k_stack[b])):
                    sp.wait_ge(s_lo, HEAD + 4 * u + 2 * side + 2)
                    for r in range(4):
                        low = r % 2 if side == 0 else r // 2
                        src = part_lo if low else part_hi
                        for h in range(GH):
                            sp.dma_start(st[32 * r:32 * r + 32, h, :].bitcast(F32),
                                         src[32 * h:32 * h + 32, side, :].bitcast(F32)).then_inc(s_stack[b], 16)

            def group(g, last):
                stack(2 * g + 1, 1)
                if not last:
                    sp.wait_ge(s_fill, HEAD + 2 * FILLS * (g + 1))
                    load_w(g + 1)
                    stack(2 * g + 2, 0)

            load_w(0)
            stack(0, 0, first=True)
            with sp.Fori(0, GROUPS - 1) as g:
                group(g, False)
            group(GROUPS - 1, True)

        def passed(pool):
            pool.sem_inc(s_passed, 1)

        def att_pool(pool):
            def split(u, b, loaded):
                for side in range(2):
                    for half in range(2):
                        c = slice(half * 512, half * 512 + 512)
                        pool.wait_ge(s_fact if side == 0 else s_fdve, HEAD + 3 * u + half + 1)
                        if loaded is not None:
                            pool.wait_ge(s_stack[1 - b], loaded)
                        passed(pool)
                        pool.tensor_copy(part_hi[:, side, c], full[:, side, :]).then_inc(s_hi, 1)
                        pool.wait_ge(s_hi, HEAD + 4 * u + 2 * side + half + 1)
                        pool.tensor_tensor(part_lo[:, side, c], full[:, side, :],
                                           part_hi[:, side, c].bitcast(F32), ALU.subtract).then_inc(s_lo, 1)

            def group(g, last):
                split(2 * g + 1, 1, STACKED * (g + 1))
                if not last:
                    split(2 * g + 2, 0, STACKED * (g + 1))

            pool.sem_inc(s_lo, HEAD)
            pool.sem_inc(s_hi, HEAD)
            split(0, 0, None)
            with pool.Fori(0, GROUPS - 1) as g:
                group(g, False)
            group(GROUPS - 1, True)

        def fill_evac(eng, who, u, f, b):
            src = bank(7)
            n = HEAD + FILLS * u + f + 1
            if f in (0, 1) and who == "act":
                eng.wait_ge(s_fill, n)
                eng.wait_ge(s_lo, HEAD + 4 * u + (f if f else -2))
                eng.activation(full[:, 0, :], src, ACT.Copy, scale=-ATT_SCALE).then_inc(s_fact, 1)
            if f in (2, 3) and who == "dve":
                eng.wait_ge(s_fill, n)
                eng.wait_ge(s_lo, HEAD + 4 * u + (3 if f == 3 else 0))
                eng.tensor_copy(full[:, 1, :], src).then_inc(s_fdve, 1)
            if f in (4, 5) and who == ("act", "dve")[f - 4]:
                eng.wait_ge(s_fill, n)
                eng.wait_ge(s_PV, HEAD + (u - 1) * QT)
                dst = v_unit[b][:, 4 * (f - 4):4 * (f - 4) + 4, :].rearrange("p a n -> p (a n)")
                if who == "act":
                    eng.copy(dst, src).then_inc(s_fact, 1)
                else:
                    eng.tensor_copy(dst, src).then_inc(s_fdve, 1)

        def att_pe(pe):
            def fill_piece(u, b, f, k, loads):
                if k == 0:
                    pe.wait_ge(s_w, loads)
                    copied, count = ((s_fdve, 0), (s_fact, 1), (s_fact, 2), (s_fdve, 1), (s_fdve, 2), (s_fact, 3))[f]
                    pe.wait_ge(copied, HEAD + 3 * u + count)
                if f < 4:
                    side, half = f // 2, f % 2
                    t0 = b * SEQ + half * 512
                    mm = pe.matmul(bank(7), w_unit[:, k, side * P:(side + 1) * P], xnT[:, k, t0:t0 + 512],
                                   start=(k == 0), stop=(k == KC - 1), skip_group_check=True)
                else:
                    t0 = b * SEQ + ((f - 4) * 4 + k) * P
                    for c in range(KC):
                        mm = pe.matmul(bank(7)[:, k * P:(k + 1) * P], xnT[:, c, t0:t0 + P],
                                       w_unit[:, c, 2 * P:3 * P], start=(c == 0), stop=(c == KC - 1))
                if k == KC - 1:
                    mm.then_inc(s_fill, 1)

            def scores(u, b, n):
                i, h = n // GH, n % GH
                pe.wait_ge(s_E, HEAD + u * STEPS + n - 1)
                dst = bank(2 * (n % 2), 2)
                width = (i + 2) // 2 * 256
                qs = q_stack[b][:, h, i * P:(i + 1) * P]
                for c0 in range(0, width, 512):
                    c1 = min(width, c0 + 512)
                    own = c0 <= i * P < c1
                    mm = pe.matmul(dst[:, c0:c1], qs, k_stack[b][:, h, c0:c1], start=True, stop=not own)
                    if own:
                        mm = pe.matmul(dst[:, i * P:(i + 1) * P], ident_bf[:, :], mask_bf[:, :], start=False,
                                       stop=True)
                mm.then_inc(s_S, 1)

            def turn(u, n):
                i, h = n // GH, n % GH
                pe.wait_ge(s_E, HEAD + u * STEPS + n + 1)
                for k in range(turned_banks(i)):
                    m = bank_no(i, h, k)
                    wait_bank_free(pe, u, m)
                    for j in range(4 * k, min(4 * k + 4, i + 1)):
                        mm = pe.transpose(bank(4 + m % 2)[:, (j - 4 * k) * P:(j - 4 * k + 1) * P],
                                          probs[n % PSLOTS][:, j * P:(j + 1) * P], ident[:, :])
                    mm.then_inc(s_T, 1)

            def heads(u, b, i):
                last = bank_no(i, GH - 1, turned_banks(i) - 1) + 1
                for e, s in (("act", s_Ca), ("dve", s_Cd)):
                    pe.wait_ge(s, HEAD + u * UCOPY[e] + copies(e, last))
                pe.wait_ge(s_AT, HEAD + u * QT + i)
                for j in range(i + 1):
                    for h in range(GH):
                        pe.matmul(bank(6)[32 * h:32 * h + 32, 0:P], v_unit[b][:, j, 32 * h:32 * h + 32],
                                  probsT[i % 2][:, h, j * P:(j + 1) * P], start=(j == 0), stop=(j == i))
                pe.wait_ge(s_Z, HEAD + u * QT + i + 1)
                pe.matmul(bank(6)[:, P:2 * P], z_inv[:, i % 2, :, :].rearrange("p h d -> p (h d)"),
                          ident[:, :], start=True, stop=True).then_inc(s_PV, 1)

            def unit(u, b, g, prev, nxt):
                for n in range(STEPS):
                    if n + 1 < STEPS:
                        scores(u, b, n + 1)
                    elif nxt:
                        first_scores(u + 1, 1 - b, g + b)
                    if n >= 1:
                        turn(u, n - 1)
                    elif prev:
                        turn(u - 1, STEPS - 1)
                    if nxt and n // 5 < FILLS and n % 5 < KC:
                        fill_piece(u + 1, 1 - b, n // 5, n % 5, 16 * (g + 1 + b))
                    if n % GH == 2:
                        if n > GH:
                            heads(u, b, n // GH - 1)
                        elif prev:
                            heads(u - 1, 1 - b, QT - 1)

            def first_scores(u, b, g):
                pe.wait_ge(s_stack[b], STACKED * (g + 1))
                pe.wait_ge(s_fact, HEAD + 3 * u + 3)
                pe.wait_ge(s_fdve, HEAD + 3 * u + 3)
                scores(u, b, 0)

            for s in (s_S, s_T, s_fill, s_PV):
                pe.sem_inc(s, HEAD)
            for f in range(FILLS):
                for k in range(KC):
                    fill_piece(0, 0, f, k, 16)
            first_scores(0, 0, 0)
            unit(0, 0, 0, False, True)
            with pe.Fori(0, GROUPS - 1) as g:
                unit(2 * g + 1, 1, g, True, True)
                unit(2 * g + 2, 0, g + 1, True, True)
            last = 2 * GROUPS - 1
            unit(last, 1, GROUPS - 1, True, False)
            turn(last, STEPS - 1)
            heads(last, 1, QT - 1)

        def copy_turned(eng, who, u, n):
            i, h = n // GH, n % GH
            for k in range(turned_banks(i)):
                if copier(i, h, k) != who:
                    continue
                m = bank_no(i, h, k)
                eng.wait_ge(s_T, HEAD + u * UB + m + 1)
                eng.wait_ge(s_PV, HEAD + u * QT + i - 1)
                c0, c1 = 4 * k * P, min(4 * k + 4, i + 1) * P
                dst, src = probsT[i % 2][:, h, c0:c1], bank(4 + m % 2)[:, 0:c1 - c0]
                if who == "act":
                    eng.copy(dst, src).then_inc(s_Ca, 1)
                else:
                    eng.tensor_copy(dst, src).then_inc(s_Cd, 1)

        def att_act(act):
            def exp(u, n):
                i, h = n // GH, n % GH
                act.wait_ge(s_M, HEAD + u * STEPS + n + 1)
                if n >= 2:
                    j, k = (n - 2) // GH, (n - 2) % GH
                    act.wait_ge(s_T, HEAD + u * UB + bank_no(j, k, turned_banks(j) - 1) + 1)
                else:
                    act.wait_ge(s_T, HEAD + u * UB - (2 if n == 0 else 0))
                act.wait_ge(s_Z, HEAD + u * QT + i - 1)
                act.activation(probs[n % PSLOTS][:, 0:(i + 1) * P], bank(2 * (n % 2), 2)[:, 0:(i + 1) * P], ACT.Exp,
                               bias=nmax[:, n % 4:n % 4 + 1], scale=-1.0,
                               accum_out=z_sum[:, i % 2, h:h + 1]).then_inc(s_E, 1)

            def z_row(u, i):
                act.wait_ge(s_PV, HEAD + u * QT + i + 1)
                act.wait_ge(s_AT, HEAD + u * QT + i - 1)
                act.copy(z_rows[:, i % 2, :], bank(6)[:, P:2 * P]).then_inc(s_ZR, 1)

            def unit(u, b, prev, nxt):
                for n in range(STEPS):
                    if n >= 2:
                        copy_turned(act, "act", u, n - 2)
                    elif prev:
                        copy_turned(act, "act", u - 1, STEPS + n - 2)
                    exp(u, n)
                    if nxt and n % 5 == 4:
                        fill_evac(act, "act", u + 1, n // 5, 1 - b)
                    if n % GH == 3:
                        if n > GH:
                            z_row(u, n // GH - 1)
                        elif prev:
                            z_row(u - 1, QT - 1)

            for s in (s_E, s_Ca, s_fact, s_ZR):
                act.sem_inc(s, HEAD)
            for f in range(FILLS):
                fill_evac(act, "act", 0, f, 0)
            unit(0, 0, False, True)
            with act.Fori(0, GROUPS - 1) as g:
                unit(2 * g + 1, 1, True, True)
                unit(2 * g + 2, 0, True, True)
            last = 2 * GROUPS - 1
            unit(last, 1, True, False)
            for n in (STEPS - 2, STEPS - 1):
                copy_turned(act, "act", last, n)
            z_row(last, QT - 1)

        def att_dve(dve):
            def row_max(u, n):
                i = n // GH
                dve.wait_ge(s_S, HEAD + u * STEPS + n + 1)
                dve.wait_ge(s_E, HEAD + u * STEPS + n - 3)
                dve.tensor_reduce(nmax[:, n % 4:n % 4 + 1], bank(2 * (n % 2), 2)[:, 0:(i + 1) * P], AX.X,
                                  ALU.min).then_inc(s_M, 1)

            def z_invert(u, i):
                dve.wait_ge(s_E, HEAD + u * STEPS + GH * i + GH)
                dve.wait_ge(s_PV, HEAD + u * QT + i - 1)
                dve.reciprocal(z_rec[:, i % 2, :], z_sum[:, i % 2, :]).then_inc(s_Zr, 1)
                dve.wait_ge(s_Zr, HEAD + u * QT + i + 1)
                dve.tensor_copy(z_inv[:, i % 2, :, :],
                                z_rec[:, i % 2, :].unsqueeze(2).to_broadcast([P, GH, HD])).then_inc(s_Z, 1)

            def normalize(u, b, i, g):
                dve.wait_ge(s_ZR, HEAD + u * QT + i + 1)
                dst = attnT[:, bass.ds(g * T + (b * SEQ + i * P), P)]
                dve.tensor_tensor(dst, bank(6)[:, 0:P], z_rows[:, i % 2, :], ALU.mult).then_inc(s_AT, 1)

            def unit(u, b, g, pg, nxt):
                for n in range(STEPS):
                    row_max(u, n)
                    if nxt and n % 5 == 4:
                        fill_evac(dve, "dve", u + 1, n // 5, 1 - b)
                    if n >= 2:
                        copy_turned(dve, "dve", u, n - 2)
                    elif pg is not None:
                        copy_turned(dve, "dve", u - 1, STEPS + n - 2)
                    if n % GH == 0:
                        if n:
                            z_invert(u, n // GH - 1)
                        elif pg is not None:
                            z_invert(u - 1, QT - 1)
                    if n % GH == 3:
                        if n > GH:
                            normalize(u, b, n // GH - 1, g)
                        elif pg is not None:
                            normalize(u - 1, 1 - b, QT - 1, pg)

            for s in (s_M, s_Cd, s_Zr, s_Z, s_AT, s_fdve):
                dve.sem_inc(s, HEAD)
            for f in range(FILLS):
                fill_evac(dve, "dve", 0, f, 0)
            unit(0, 0, 0, None, True)
            with dve.Fori(0, GROUPS - 1) as g:
                unit(2 * g + 1, 1, g, g, True)
                unit(2 * g + 2, 0, g + 1, g, True)
            last = 2 * GROUPS - 1
            unit(last, 1, GROUPS - 1, GROUPS - 1, False)
            for n in (STEPS - 2, STEPS - 1):
                copy_turned(dve, "dve", last, n)
            z_invert(last, QT - 1)
            normalize(last, 1, QT - 1, GROUPS - 1)

        def inv_std(pool, c):
            pool.wait_ge(s_var, c + 1)
            if c >= 2:
                pool.wait_ge(s_xn, c - 1)
            pool.tensor_tensor(rstd[:, c % 2:c % 2 + 1], mv[:, c % 2, 1:2], half_neg[:, :],
                               ALU.pow).then_inc(s_rstd, 1)

        ATT_DONE = HEAD + 2 * GROUPS * QT
        LAST = TILES - 1
        SHARED = NT
        PLANNED = 5


        def moe_sp(sp):
            for q in range(RING):
                sp.wait_ge(s_hst[q], 16 * (NT // RING))
            sp.wait_ge(s_AT, ATT_DONE)
            sp.dma_start(wo[:, :, :], a["woT"]).then_inc(s_wo, 16)
            for c in range(NT):
                sp.dma_start(acc[:, c, :], h_dram[c * P:(c + 1) * P, :]).then_inc(s_hl[c], 16)
            sp.dma_start(wr[:, :, :], a["wrT"]).then_inc(s_rtw, 16)
            sp.dma_start(bias[:, :], a["bias"]).then_inc(s_rtw, 16)
            sp.dma_start(w_sgu[:, :, :], a["sgu"]).then_inc(s_sw, 16)
            sp.dma_start(w_sd[:, :, :], a["sd"]).then_inc(s_sw, 16)
            for c in range(NT):
                sp.wait_ge(s_xn2, c + 1)
                sp.dma_start(xn2_dram[c * P:(c + 1) * P, :], xn2[:, c % 2, :]).then_inc(s_xst[c % 2], 16)

            def load(e, s):
                src_gu = a["wgu"][bass.ds(e, 1), :, :, :].rearrange("o p k n -> (o p) k n")
                src_dn = a["wd"][bass.ds(e, 1), :, :, :].rearrange("o p k n -> (o p) k n")
                sp.dma_start(w_gu[:, s, :, :], src_gu).then_inc(s_wl[s], 16)
                sp.dma_start(w_dn[:, s, :, :], src_dn).then_inc(s_wl[s], 16)

            def ready(m, s):
                sp.wait_ge(s_wl[s], 32 * (m + 1))
                sp.sem_inc(s_wr, 1)

            def store(c):
                sp.wait_ge(s_acc, c + 1)
                sp.dma_start(out[c * P:(c + 1) * P, :], acc[:, c, :]).then_inc(s_out[c], 16)

            sp.wait_ge(s_op, NT)
            for s in range(WRING):
                load(s, s)
            for s in range(WRING):
                ready(0, s)
            for c in range(NT):
                store(c)
            sp.dma_start(out[T:T + P, :], acc[:, 0, :]).then_inc(s_pad, 16)
            sp.wait_ge(s_plan, PLANNED)
            with sp.Fori(1, E // WRING) as m:
                for s in range(WRING):
                    done = sp.value_load(tiles_to_i[0:1, bass.ds(WRING * m + (s - WRING), 1)], min_val=0,
                                         max_val=TILES)
                    sp.wait_ge(s_y, done + SHARED)
                    load(WRING * m + s, s)
                    ready(m, s)
            sp.wait_ge(s_yadd, 16 * TILES)

        def moe_pool(pool):
            for c in range(NT):
                pool.wait_ge(s_var2, c + 1)
                if c >= 2:
                    pool.wait_ge(s_xn2, c - 1)
                pool.tensor_tensor(rstd2[:, c % 2:c % 2 + 1], mv2[:, c % 2, 1:2], half_neg[:, :],
                                   ALU.pow).then_inc(s_rstd2, 1)
            for s in range(2):
                pool.wait_ge(s_xst[s], 16 * (NT // 2))
            pool.wait_ge(s_plan, PLANNED)

            def gather(m, s, first):
                if not first:
                    pool.wait_ge(s_xT2, 2 * m + (s - 1))
                    pool.wait_ge(s_xg[s], 16 * m)
                    passed(pool)
                pool.tensor_copy(rows_no[s][:, :], slot_tok[:, bass.ds(2 * m + s, 1)]).then_inc(s_rn, 1)
                pool.wait_ge(s_rn, 2 * m + (s + 1))
                passed(pool)
                pool.indirect_dma_start(
                    out=x_rows[s][:, :], out_offset=None, in_=xn2_dram,
                    in_offset=bass.IndirectOffsetOnAxis(ap=rows_no[s][:, :], axis=0),
                    bounds_check=T - 1, oob_is_err=False).then_inc(s_xg[s], 16)

            def add(m, s, first):
                pool.wait_ge(s_yc, 2 * m + (s + 1))
                if not first:
                    pool.wait_ge(s_yadd, 16 * (2 * m + s))
                passed(pool)
                pool.tensor_copy(out_no[s][:, :], slot_out[:, bass.ds(2 * m + s, 1)]).then_inc(s_on, 1)
                pool.wait_ge(s_on, 2 * m + (s + 1))
                passed(pool)
                pool.indirect_dma_start(
                    out=out, out_offset=bass.IndirectOffsetOnAxis(ap=out_no[s][:, :], axis=0),
                    in_=y_sb[:, s, :], in_offset=None, bounds_check=T + P - 1, oob_is_err=True,
                    compute_op=ALU.add).then_inc(s_yadd, 16)

            gather(0, 0, True)
            gather(0, 1, True)
            gather(1, 0, False)
            gather(1, 1, False)
            for c in range(NT):
                pool.wait_ge(s_out[c], 16)
            pool.wait_ge(s_pad, 16)
            passed(pool)
            add(0, 0, True)
            with pool.Fori(2, TILES // 2) as m:
                gather(m, 0, False)
                add(m - 2, 1, False)
                gather(m, 1, False)
                add(m - 1, 0, False)
            for j in range(TILES - 3, TILES):
                add(j // 2, j % 2, False)

        def moe_act(act):
            for c in range(NT):
                act.wait_ge(s_x2T, c + 1)
                if c == 0:
                    act.wait_ge(s_AT, ATT_DONE)
                act.copy(xnT[:, :, c * P:(c + 1) * P],
                         bank(2 + c % 2).rearrange("p (k n) -> p k n", k=KC)).then_inc(s_x2C, 1)
            act.wait_ge(s_shift, 1)
            act.activation(probs_e[:, :, :], logits[:, :, :], ACT.Exp).then_inc(s_exp, 1)

            def silu(n, p):
                act.wait_ge(s_gu, n + 1)
                if not isinstance(n, int) or n >= 2:
                    act.wait_ge(s_gated, n - 1)
                act.activation(silu_g[:, p, :], bank(2 + p)[:, 0:FF], ACT.Silu).then_inc(s_silu, 1)

            def turn_copy(n, p):
                act.wait_ge(s_gT, n + 1)
                if not isinstance(n, int) or n >= 2:
                    act.wait_ge(s_y, n - 1)
                act.copy(gated_T[:, p, :], bank(4 + p)[:, 0:FF]).then_inc(s_gC, 1)

            for n in range(SHARED):
                if n >= 1:
                    turn_copy(n - 1, (n - 1) % 2)
                silu(n, n % 2)

            def routed(m, s, first, added):
                n = SHARED + 2 * m + s
                q = 1 - s
                turn_copy(n - 1, q)
                silu(n, s)
                if not first:
                    y_scale(n - 1, q, added)

            def y_scale(n, q, added):
                act.wait_ge(s_y, n + 1)
                if added is not None:
                    act.wait_ge(s_yadd, added)
                act.activation(y_sb[:, q, :], bank(6 + q), ACT.Copy,
                               scale=slot_w[:, bass.ds(n - SHARED, 1)]).then_inc(s_yc, 1)

            routed(0, 0, True, None)
            routed(0, 1, False, None)
            routed(1, 0, False, None)
            routed(1, 1, False, 16)
            with act.Fori(2, TILES // 2) as m:
                routed(m, 0, False, 16 * (2 * m - 2))
                routed(m, 1, False, 16 * (2 * m - 1))
            turn_copy(SHARED + LAST, 1)
            y_scale(SHARED + LAST, 1, 16 * (LAST - 1))

        def moe_dve(dve):
            step = Chain(dve, s_dve2)

            def residual(c):
                s = c % 2
                dve.wait_ge(s_op, c + 1)
                dve.wait_ge(s_hl[c], 16)
                step(dve.tensor_tensor(acc[:, c, :], acc[:, c, :], bank(s), ALU.add))
                step(dve.bn_stats(stats2[:, s, :], acc[:, c, :]))
                step(dve.bn_aggr(mv2[:, s, :], stats2[:, s, :]))
                dve.tensor_scalar(mv2[:, s, 1:2], mv2[:, s, 1:2], LN_EPS, None, ALU.add).then_inc(s_var2, 1)

            def norm2(c):
                s = c % 2
                dve.wait_ge(s_rstd2, c + 1)
                if c >= 2:
                    dve.wait_ge(s_x2T, c - 1)
                    dve.wait_ge(s_xst[s], 16 * (c // 2))
                dve.tensor_scalar(xn2[:, s, :], acc[:, c, :], mv2[:, s, 0:1], rstd2[:, s:s + 1],
                                  ALU.subtract, ALU.mult).then_inc(s_xn2, 1)

            def logit(c):
                dve.wait_ge(s_lg, c + 1)
                if c == 0:
                    dve.wait_ge(s_rtw, 32)
                dve.tensor_tensor(logits[:, c, :], bank(4 + c % 2)[:, 0:E], bias[:, :], ALU.add).then_inc(s_lgc, 1)

            for c in range(NT + 3):
                if c < NT:
                    residual(c)
                if 1 <= c <= NT:
                    norm2(c - 1)
                if c >= 3:
                    logit(c - 3)

            def over_e(x):
                return x.unsqueeze(2).to_broadcast([P, NT, E])

            def router_shift():
                dve.wait_ge(s_lgc, NT)
                step(dve.tensor_reduce(row_red[:, :], logits[:, :, :], AX.X, ALU.max))
                dve.tensor_tensor(logits[:, :, :], logits[:, :, :], over_e(row_red[:, :]),
                                  ALU.subtract).then_inc(s_shift, 1)

            def router_probs():
                dve.wait_ge(s_exp, 1)
                step(dve.tensor_reduce(row_red[:, :], probs_e[:, :, :], AX.X, ALU.add))
                step(dve.reciprocal(row_red[:, :], row_red[:, :]))
                step(dve.tensor_tensor(probs_e[:, :, :], probs_e[:, :, :], over_e(row_red[:, :]), ALU.mult))

            def top2(c0, c1):
                for c in range(c0, c1):
                    step(dve.max(top_v[:, c, :], probs_e[:, c, :]))
                    step(dve.max_index(top_i[:, c, :], top_v[:, c, :], probs_e[:, c, :]))

            def weights():
                step(dve.tensor_tensor(w_sum[:, :], top_v[:, :, 0], top_v[:, :, 1], ALU.add))
                step(dve.tensor_scalar(w_sum[:, :], w_sum[:, :], W_EPS, None, ALU.add))
                step(dve.reciprocal(w_sum[:, :], w_sum[:, :]))
                step(dve.tensor_tensor(w_top[:, :, :], top_v[:, :, 0:TOPK],
                                       w_sum[:, :].unsqueeze(2).to_broadcast([P, NT, TOPK]), ALU.mult))
                step(dve.tensor_copy(top_f[:, :, :], top_i[:, :, 0:TOPK]))
                for k in range(TOPK):
                    step(dve.tensor_tensor(oh_e[:, k, :, :], iota_e[:, :].unsqueeze(1).to_broadcast([P, NT, E]),
                                           over_e(top_f[:, :, k]), ALU.is_equal))
                dve.tensor_tensor(oh_any[:, :, :], oh_e[:, 0, :, :], oh_e[:, 1, :, :], ALU.add).then_inc(s_oh, 1)

            def places():
                dve.wait_ge(s_rank, 1)
                step(dve.tensor_copy(count_e[:, :], bank(0)[:, NT * E:NT * E + E]))
                ee = [P, E, E]
                step(dve.tensor_tensor(cmp_e[:, :, :], count_e[:, :].unsqueeze(2).to_broadcast(ee),
                                       iota_p128[:, :].unsqueeze(1).to_broadcast(ee), ALU.is_gt))
                step(dve.tensor_reduce(tiles_e[:, :], cmp_e[:, :, :], AX.X, ALU.add))
                step(dve.tensor_scalar(tiles_e[:, :], tiles_e[:, :], 1.0, None, ALU.max))
                step(dve.tensor_tensor(cmp_e[:, :, :], tiles_e[:, :].unsqueeze(1).to_broadcast(ee),
                                       upto_e[:, :, :], ALU.mult))
                step(dve.tensor_reduce(tiles_to[:, :], cmp_e[:, :, :], AX.X, ALU.add))
                step(dve.tensor_tensor(base_e[:, :], tiles_to[:, :], tiles_e[:, :], ALU.subtract))
                step(dve.tensor_scalar(base_e[:, :], base_e[:, :], float(P), None, ALU.mult))
                dve.tensor_copy(tiles_to_i[:, :], tiles_to[:, :]).then_inc(s_plan, 1)
                rank = bank(0)[:, 0:NT * E].rearrange("p (c e) -> p c e", e=E)
                step(dve.tensor_tensor(pos_all[:, :, :], rank, base_e[:, :].unsqueeze(1).to_broadcast([P, NT, E]),
                                       ALU.add))
                for k in range(TOPK):
                    step(dve.tensor_tensor(pos_pick[:, :, :], oh_e[:, k, :, :], pos_all[:, :, :], ALU.mult))
                    step(dve.tensor_reduce(pos_f[:, k, :], pos_pick[:, :, :], AX.X, ALU.add))
                step(dve.tensor_copy(pos_i[:, :, :], pos_f[:, :, :]))
                step(dve.tensor_scalar(pos_hl[:, 0, :, :], pos_i[:, :, :], 7, None, ALU.arith_shift_right))
                step(dve.tensor_scalar(pos_hl[:, 1, :, :], pos_i[:, :, :], P - 1, None, ALU.bitwise_and))
                step(dve.tensor_copy(pos_hlf[:, :, :, :], pos_hl[:, :, :, :]))

            def tile_experts():
                je = [P, TILES, E]
                step(dve.tensor_tensor(cmp_j[:, :, :], tiles_to[:, :].unsqueeze(1).to_broadcast(je),
                                       iota_j[:, :].unsqueeze(2).to_broadcast(je), ALU.is_le))
                step(dve.tensor_reduce(tile_e[:, :], cmp_j[:, :, :], AX.X, ALU.add))
                dve.tensor_scalar(tile_e_i[:, :], tile_e[:, :], float(E - 1), None, ALU.min).then_inc(s_plan, 1)

            def slot_onehots(n0, n1):
                for n in range(n0, n1):
                    c, k, r = n // TOPK, n % TOPK, n % 4
                    if n >= 4:
                        dve.wait_ge(s_slotm, n - 3)
                    dve.tensor_scalar(slot_lo[:, r, :], iota_f[:, :], pos_hlf[:, 1, k, c:c + 1], None,
                                      ALU.is_equal).then_inc(s_slot, 1)
                    dve.tensor_scalar(slot_hi[:, r, 0, :], iota_j[:, :], pos_hlf[:, 0, k, c:c + 1],
                                      tok_no1[:, c:c + 1], ALU.is_equal, ALU.mult).then_inc(s_slot, 1)
                    dve.tensor_scalar(slot_hi[:, r, 1, :], iota_j[:, :], pos_hlf[:, 0, k, c:c + 1],
                                      w_top[:, c, k:k + 1], ALU.is_equal, ALU.mult).then_inc(s_slot, 1)

            def slot_tokens():
                dve.wait_ge(s_slotm, TOPK * NT)
                dve.tensor_copy(slot_w[:, :], bank(1)[:, TILES:2 * TILES]).then_inc(s_plan, 1)
                step(dve.tensor_scalar(slot_f[:, :], bank(1)[:, 0:TILES], -1.0, None, ALU.add))
                dve.tensor_scalar(slot_tok[:, :], slot_f[:, :], 0.0, None, ALU.max).then_inc(s_plan, 1)
                step(dve.tensor_scalar(pad_row[:, :], tok_no1[:, 0:1], float(T), None, ALU.add))
                step(dve.tensor_scalar(slot_pad[:, :], slot_f[:, :], 0.0, pad_row[:, :], ALU.is_lt, ALU.mult))
                dve.tensor_tensor(slot_out[:, :], slot_pad[:, :], slot_f[:, :], ALU.add).then_inc(s_plan, 1)

            def gate(n, p):
                dve.wait_ge(s_silu, n + 1)
                if not isinstance(n, int) or n >= 2:
                    dve.wait_ge(s_gT, n - 1)
                dve.tensor_tensor(gated[:, p, :], silu_g[:, p, :], bank(2 + p)[:, FF:2 * FF],
                                  ALU.mult).then_inc(s_gated, 1)

            def shared_add(c):
                dve.wait_ge(s_y, c + 1)
                dve.tensor_tensor(acc[:, c, :], acc[:, c, :], bank(6 + c % 2), ALU.add).then_inc(s_acc, 1)

            router_shift()
            dve.wait_ge(s_moec, 7)
            for n in range(SHARED):
                gate(n, n % 2)
                if n >= 1:
                    shared_add(n - 1)
                if n == 0:
                    router_probs()
                if n < 4:
                    top2(4 * n, 4 * n + 4)
                if n == 4:
                    weights()
                if n == 6:
                    places()
                if n == 7:
                    tile_experts()
                if n >= 8:
                    slot_onehots(4 * (n - 8), 4 * (n - 8) + 4)

            def row_copy(m, s, first):
                dve.wait_ge(s_xT2, 2 * m + (s + 1))
                if not first:
                    dve.wait_ge(s_gu, SHARED + 2 * m + (s - 1))
                dve.tensor_copy(x_T[:, s, :], bank(s)).then_inc(s_xC2, 1)

            slot_tokens()
            row_copy(0, 0, True)
            shared_add(SHARED - 1)
            row_copy(0, 1, True)
            gate(SHARED, 0)
            with dve.Fori(1, TILES // 2) as m:
                row_copy(m, 0, False)
                gate(SHARED + 2 * m - 1, 1)
                row_copy(m, 1, False)
                gate(SHARED + 2 * m, 0)
            gate(SHARED + LAST, 1)

        def moe_pe(pe):
            pe.wait_ge(s_AT, ATT_DONE)
            pe.wait_ge(s_wo, 16)
            for c in range(NT + 3):
                if c < NT:
                    if c >= 2:
                        pe.wait_ge(s_var2, c - 1)
                    for g in range(GROUPS):
                        mm = pe.matmul(bank(c % 2), attnT[:, g * T + c * P:g * T + (c + 1) * P], wo[:, g, :],
                                       start=(g == 0), stop=(g == GROUPS - 1))
                    mm.then_inc(s_op, 1)
                if 2 <= c <= NT + 1:
                    t = c - 2
                    pe.wait_ge(s_xn2, t + 1)
                    if t >= 2:
                        pe.wait_ge(s_x2C, t - 1)
                    for k in range(KC):
                        mm = pe.transpose(bank(2 + t % 2)[:, k * P:(k + 1) * P], xn2[:, t % 2, k * P:(k + 1) * P],
                                          ident[:, :])
                    mm.then_inc(s_x2T, 1)
                if c >= 3:
                    t = c - 3
                    if t == 0:
                        pe.wait_ge(s_rtw, 32)
                    pe.wait_ge(s_x2C, t + 1)
                    if t >= 2:
                        pe.wait_ge(s_lgc, t - 1)
                    for k in range(KC):
                        mm = pe.matmul(bank(4 + t % 2)[:, 0:E], xnT[:, k, t * P:(t + 1) * P], wr[:, k, :],
                                       start=(k == 0), stop=(k == KC - 1))
                    mm.then_inc(s_lg, 1)

            def ranks():
                pe.wait_ge(s_oh, 1)
                b = bank(0)
                flat = oh_any[:, :, :].rearrange("p c e -> p (c e)")
                pe.matmul(b[:, 0:NT * E], tri_bf[:, :], flat, start=True, stop=False, skip_group_check=True)
                for c in range(NT):
                    if c < NT - 1:
                        pe.matmul(b[:, (c + 1) * E:NT * E].rearrange("p (c e) -> p c e", e=E), ones_bf[:, :],
                                  oh_any[:, c, :].unsqueeze(1).to_broadcast([P, NT - 1 - c, E]),
                                  start=False, stop=False, skip_group_check=True)
                    mm = pe.matmul(b[:, NT * E:NT * E + E], ones_bf[:, :], oh_any[:, c, :], start=False,
                                   stop=(c == NT - 1), skip_group_check=True)
                mm.then_inc(s_rank, 1)

            def slots(n0, n1):
                for n in range(n0, n1):
                    pe.wait_ge(s_slot, 3 * n + 3)
                    pe.matmul(bank(1)[:, 0:2 * TILES], slot_lo[:, n % 4, :],
                              slot_hi[:, n % 4, :, :].rearrange("p a n -> p (a n)"), start=(n == 0),
                              stop=(n == TOPK * NT - 1), skip_group_check=True).then_inc(s_slotm, 1)

            def gate_up(n, p, k0, k1, lhs, rhs):
                if k0 == 0 and (not isinstance(n, int) or n >= 2):
                    pe.wait_ge(s_gated, n - 1)
                for k in range(k0, k1):
                    mm = pe.matmul(bank(2 + p), lhs(k), rhs(k), start=(k == 0), stop=(k == KC - 1),
                                   skip_group_check=True)
                if k1 == KC:
                    mm.then_inc(s_gu, 1)

            def turn_gated(n, p):
                pe.wait_ge(s_gated, n + 1)
                if not isinstance(n, int) or n >= 2:
                    pe.wait_ge(s_gC, n - 1)
                for k in range(2):
                    mm = pe.transpose(bank(4 + p)[:, k * P:(k + 1) * P], gated[:, p, k * P:(k + 1) * P], ident[:, :])
                mm.then_inc(s_gT, 1)

            def down(n, p, rhs, freed):
                pe.wait_ge(s_gC, n + 1)
                if freed is not None:
                    pe.wait_ge(*freed)
                for k in range(2):
                    mm = pe.matmul(bank(6 + p), gated_T[:, p, k * P:(k + 1) * P], rhs(k), start=(k == 0),
                                   stop=(k == 1))
                mm.then_inc(s_y, 1)

            pe.wait_ge(s_sw, 32)
            for n in range(SHARED):
                lhs = lambda k: xnT[:, k, n * P:(n + 1) * P]
                rhs = lambda k: w_sgu[:, k, :]
                gate_up(n, n % 2, 0, 2, lhs, rhs)
                if n >= 1:
                    turn_gated(n - 1, (n - 1) % 2)
                gate_up(n, n % 2, 2, KC, lhs, rhs)
                if n >= 1:
                    down(n - 1, (n - 1) % 2, lambda k: w_sd[:, k, :], (s_acc, n - 2) if n >= 3 else None)
                if n == 5:
                    ranks()
                if n >= 9:
                    slots(4 * (n - 9), 4 * (n - 9) + 4)
            slots(4 * (SHARED - 9), TOPK * NT)

            def turn_rows(m, s, first):
                pe.wait_ge(s_xg[s], 16 * (m + 1))
                if not first:
                    pe.wait_ge(s_xC2, 2 * m + (s - 1))
                for k in range(KC):
                    mm = pe.transpose(bank(s)[:, k * P:(k + 1) * P], x_rows[s][:, k * P:(k + 1) * P], ident[:, :])
                mm.then_inc(s_xT2, 1)

            def routed(m, s, before, after):
                n = SHARED + 2 * m + s
                e = pe.value_load(tile_e_i[0:1, bass.ds(2 * m + s, 1)], min_val=0, max_val=E - 1)
                half = pe.snap(e % WRING)
                half_before = expert_half(2 * m + (s - 1)) if before else None
                pe.wait_ge(s_wr, e + 1)
                pe.wait_ge(s_xC2, 2 * m + (s + 1))
                lhs = lambda k: x_T[:, s, k * P:(k + 1) * P]
                rhs = lambda k: w_gu[:, bass.ds(half, 1), k, :].rearrange("p o n -> p (o n)")
                gate_up(n, s, 0, 2, lhs, rhs)
                turn_gated(n - 1, 1 - s)
                gate_up(n, s, 2, KC, lhs, rhs)
                if after is not None:
                    turn_rows(*after)
                if before:
                    down_of(n - 1, 1 - s, 2 * m + (s - 1), half_before)
                else:
                    down(n - 1, 1 - s, lambda k: w_sd[:, k, :], (s_acc, n - 2))

            def expert_half(j):
                e = pe.value_load(tile_e_i[0:1, bass.ds(j, 1)], min_val=0, max_val=E - 1)
                return pe.snap(e % WRING)

            def down_of(n, p, j, half):
                pe.wait_ge(s_gC, n + 1)
                if isinstance(j, int) and j < 2:
                    pe.wait_ge(s_acc, SHARED + j - 1)
                else:
                    pe.wait_ge(s_yc, j - 1)
                for k in range(2):
                    mm = pe.matmul(bank(6 + p), gated_T[:, p, k * P:(k + 1) * P],
                                   w_dn[:, bass.ds(half, 1), k, :].rearrange("p o n -> p (o n)"), start=(k == 0),
                                   stop=(k == 1))
                mm.then_inc(s_y, 1)

            pe.wait_ge(s_plan, PLANNED)
            turn_rows(0, 0, True)
            routed(0, 0, False, (0, 1, True))
            routed(0, 1, True, (1, 0, False))
            routed(1, 0, True, (1, 1, False))
            with pe.Fori(2, TILES // 2) as m:
                routed(m - 1, 1, True, (m, 0, False))
                routed(m, 0, True, (m, 1, False))
            routed(TILES // 2 - 1, 1, True, None)
            turn_gated(SHARED + LAST, 1)
            down_of(SHARED + LAST, 1, LAST, expert_half(LAST))


        @block.sync
        def _(sp):
            sp.dma_start(hot_ids[:, :], a["hot_ids"]).then_inc(s_in, 16)
            sp.dma_start(tok_ids[:, :], a["tok_ids"]).then_inc(s_in, 16)
            sp.dma_start(projT[:, :], a["projT"]).then_inc(s_proj, 16)
            for c in range(NT):
                sp.wait_ge(s_h, c + 1)
                sp.dma_start(h_dram[c * P:(c + 1) * P, :], hot_vec[c % RING][:, :]).then_inc(s_hst[c % RING], 16)
            att_sp(sp)
            moe_sp(sp)

        @block.gpsimd
        def _(pool):
            step = Chain(pool, s_pool)
            for m, v in ((ident, 0.0), (ident_bf, 0.0), (tri_bf, 1.0), (mask_bf, 0.0)):
                pool.memset(m[:, :], v).then_inc(s_pool, 1)
            pool.memset(ones_bf[:, :], 1.0).then_inc(s_const, 1)
            pool.memset(half_neg[:, :], -0.5).then_inc(s_const, 1)
            pool.iota(iota_bf[:, :], pattern=[[1, 256]], base=0, channel_multiplier=0,
                      allow_small_or_imprecise_dtypes=True).then_inc(s_const, 1)
            pool.iota(row64[:, :], pattern=[[0, 1]], base=0, channel_multiplier=HOT_C,
                      allow_small_or_imprecise_dtypes=True).then_inc(s_const, 1)
            pool.iota(chunk1[:, :], pattern=[[1, HOT_C]], base=1, channel_multiplier=0,
                      allow_small_or_imprecise_dtypes=True).then_inc(s_const, 1)
            for m, pattern, base, rows in (
                    (iota_e, [[1, E]], 0, 0), (iota_p128, [[P, T // P]], 0, 0), (iota_j, [[1, TILES]], 0, 0),
                    (iota_f, [[1, P]], 0, 0), (tok_no1, [[P, NT]], 1, 1)):
                pool.iota(m[:, :], pattern=pattern, base=base, channel_multiplier=rows,
                          allow_small_or_imprecise_dtypes=True).then_inc(s_moec, 1)
            pool.memset(upto_e[:, :, :], 1.0).then_inc(s_moec, 1)
            pool.wait_ge(s_moec, 6)
            pool.affine_select(out=upto_e[:, :, :], in_=upto_e[:, :, :], compare_op=ALU.is_ge, fill=0.0, base=0,
                               pattern=[[1, E], [-1, E]], channel_multiplier=0).then_inc(s_moec, 1)
            pool.wait_ge(s_pool, 4)
            for m in (ident, ident_bf):
                pool.affine_select(out=m[:, :], in_=m[:, :], compare_op=ALU.not_equal, fill=1.0, base=0,
                                   pattern=[[-1, P]], channel_multiplier=1).then_inc(s_const, 1)
            pool.affine_select(out=tri_bf[:, :], in_=tri_bf[:, :], compare_op=ALU.is_gt, fill=0.0, base=0,
                               pattern=[[1, P]], channel_multiplier=-1).then_inc(s_const, 1)
            pool.affine_select(out=mask_bf[:, :], in_=mask_bf[:, :], compare_op=ALU.is_ge, fill=1e9, base=0,
                               pattern=[[-1, P]], channel_multiplier=1).then_inc(s_const, 1)
            zeroed = 4
            for c in range(NT):
                if c >= RING:
                    pool.wait_ge(s_hst[c % RING], 16 * (c // RING))
                    pool.wait_ge(s_xn, c - RING + 1)
                    pool.wait_ge(s_coldT, c - RING + 1)
                pool.memset(hot_vec[c % RING][:, :], 0.0).then_inc(s_pool, 1)
                pool.memset(cold_lat[c % RING][:, :], 0.0).then_inc(s_pool, 1)
                zeroed += 2
                pool.wait_ge(s_pool, zeroed)
                pool.wait_ge(s_rows, c // PER + 1)
                pool.indirect_dma_start(
                    out=cold_lat[c % RING][:, :], out_offset=None, in_=a["cold_emb"],
                    in_offset=bass.IndirectOffsetOnAxis(ap=cold_row[:, c:c + 1], axis=0),
                    bounds_check=NUM_COLD - 1, oob_is_err=False).then_inc(s_coldg[c % RING], 16)
                pool.indirect_dma_start(
                    out=hot_vec[c % RING][:, :], out_offset=None, in_=a["hot_emb"],
                    in_offset=bass.IndirectOffsetOnAxis(ap=hot_row[:, c:c + 1], axis=0),
                    bounds_check=NUM_HOT - 1, oob_is_err=False).then_inc(s_hotg[c % RING], 16)
                if c >= LAG:
                    inv_std(pool, c - LAG)
            for c in range(NT - LAG, NT):
                inv_std(pool, c)
            att_pool(pool)
            moe_pool(pool)

        @block.scalar
        def _(act):
            act.wait_ge(s_const, 9)
            for c in range(HOT_C):
                act.wait_ge(s_ohhi, c + 1)
                act.activation(oh_hi_row[:, c, :], oh_hi[:, c, :], ACT.Copy, scale=row64[:, :]).then_inc(s_row, 1)
            for k in range(2):
                act.wait_ge(s_tohT, k + 1)
                act.copy(tok_ohT[:, 8 * k:8 * k + 8, :].rearrange("p a n -> p (a n)"),
                         bank(2 + k).bitcast(BF16)[0:HI, :]).then_inc(s_tohC, 1)
            for c in range(NT + 3):
                if c < NT:
                    act.wait_ge(s_coldT, c + 1)
                    if c >= 2:
                        act.wait_ge(s_cvec, c - 1)
                    act.copy(cold_T[:, c % 2, :], bank(6 if c % 2 else 0)[:, 0:P]).then_inc(s_coldC, 1)
                if c >= 3:
                    t = c - 3
                    act.wait_ge(s_xT, t + 1)
                    act.copy(xnT[:, :, t * P:(t + 1) * P],
                             bank(2 + t % 2).rearrange("p (k n) -> p k n", k=KC)).then_inc(s_xC, 1)
            att_act(act)
            moe_act(act)

        @block.vector
        def _(dve):
            step = Chain(dve, s_dve)
            dve.wait_ge(s_in, 32)
            dve.wait_ge(s_const, 9)

            def split_ids(raw, f, wrap, ints, hi, lo, clamp):
                step(dve.tensor_copy(f[:, :], raw[:, :]))
                step(dve.tensor_scalar(wrap[:, :], f[:, :], 0.0, float(VOCAB), ALU.is_lt, ALU.mult))
                step(dve.tensor_tensor(f[:, :], f[:, :], wrap[:, :], ALU.add))
                if clamp:
                    step(dve.tensor_scalar(f[:, :], f[:, :], 0.0, float(VOCAB - 1), ALU.max, ALU.min))
                step(dve.tensor_copy(ints[:, 0, :], f[:, :]))
                step(dve.tensor_scalar(ints[:, 1, :], ints[:, 0, :], 255, None, ALU.bitwise_and))
                step(dve.tensor_copy(lo[:, :], ints[:, 1, :]))
                step(dve.tensor_scalar(ints[:, 0, :], ints[:, 0, :], 8, None, ALU.arith_shift_right))
                step(dve.tensor_copy(hi[:, :], ints[:, 0, :]))

            split_ids(hot_ids, hot_f, hot_wrap, hot_i, hot_hi, hot_lo, False)
            for c in range(HOT_C):
                dve.tensor_scalar(oh_hi[:, c, :], iota_bf[0:HOT_P, 0:HI], hot_hi[:, c:c + 1], None,
                                  ALU.is_equal).then_inc(s_ohhi, 1)
                dve.tensor_scalar(oh_lo[:, c, 0, :], iota_bf[0:HOT_P, :], hot_lo[:, c:c + 1], None,
                                  ALU.is_equal).then_inc(s_ohlo, 1)
                dve.tensor_scalar(oh_lo[:, c, 1, :], iota_bf[0:HOT_P, :], hot_lo[:, c:c + 1], chunk1[:, c:c + 1],
                                  ALU.is_equal, ALU.mult).then_inc(s_chunk, 1)
            split_ids(tok_ids, tok_f, tok_wrap, tok_i, tok_hi, tok_lo, True)
            for c in range(NT):
                dve.tensor_scalar(tok_oh[:, c, :], iota_bf[:, 0:HI], tok_hi[:, c:c + 1], None,
                                  ALU.is_equal).then_inc(s_toh, 1)
            dve.wait_ge(s_table, 1)
            tb = bank(0)
            step(dve.tensor_scalar(seen[:, :], tb[0:HI, 0:256], 1.0, None, ALU.min))
            step(dve.tensor_reduce(seen_n[:, :], seen[:, :], AX.X, ALU.add))
            dve.tensor_copy(seen_b[:, :], seen_n[:, :]).then_inc(s_seen, 1)
            step(dve.tensor_scalar(rank_i[:, 0, :], tb[0:HI, 256:512], float(NUM_HOT), None, ALU.min))
            step(dve.tensor_scalar(rank_i[:, 1, :], rank_i[:, 0, :], ~127, None, ALU.bitwise_and))
            step(dve.tensor_copy(tab_a[:, 256:512], rank_i[:, 1, :]))
            step(dve.tensor_scalar(rank_i[:, 1, :], rank_i[:, 0, :], 127, None, ALU.bitwise_and))
            step(dve.tensor_copy(tab_b[:, :], rank_i[:, 1, :]))
            dve.wait_ge(s_base, 1)
            step(dve.tensor_copy(rank_i[:, 0, 0:1], bank(1)[0:HI, 0:1]))
            step(dve.tensor_scalar(rank_i[:, 1, 0:1], rank_i[:, 0, 0:1], 127, None, ALU.bitwise_and))
            step(dve.tensor_scalar(rank_i[:, 2, 0:1], rank_i[:, 0, 0:1], ~127, None, ALU.bitwise_and))
            step(dve.tensor_copy(tab_c[:, :], rank_i[:, 2, 0:1]))
            step(dve.tensor_tensor(seen[:, 0:1], seen[:, 0:1], rank_i[:, 1, 0:1], ALU.add))
            dve.tensor_copy(tab_a[:, 0:256], seen[:, :]).then_inc(s_tab, 1)

            def look_up(c):
                s = c % 2
                if c >= 2:
                    dve.wait_ge(s_looked, 2 * (c - 1))
                dve.tensor_scalar(pick[:, s, 0, :], iota_bf[:, :], tok_lo[:, c:c + 1], None,
                                  ALU.is_le).then_inc(s_dve, 1)
                step.n += 1
                step(dve.tensor_scalar(pick[:, s, 1, :], iota_bf[:, :], tok_lo[:, c:c + 1], None, ALU.is_equal))
                dve.wait_ge(s_look, c + 1)
                dve.tensor_tensor_reduce(prod[:, s, 0, :], pick[:, s, 0, :], bank(4 + s)[:, 0:256], 1.0, 0.0,
                                         ALU.mult, ALU.add, below[:, c:c + 1]).then_inc(s_looked, 1)
                dve.tensor_tensor_reduce(prod[:, s, 1, :], pick[:, s, 1, :], bank(4 + s)[:, 256:512], 1.0, 0.0,
                                         ALU.mult, ALU.add, hot_no[:, c:c + 1]).then_inc(s_looked, 1)

            def row_numbers(k):
                r = slice(k * PER, (k + 1) * PER)
                dve.wait_ge(s_looked, 2 * (k + 1) * PER)
                step(dve.tensor_scalar(tmp_a[:, r], hot_no[:, r], 0.0, SKIP, ALU.is_equal, ALU.mult))
                step(dve.tensor_tensor(tmp_a[:, r], tmp_a[:, r], hot_no[:, r], ALU.add))
                dve.tensor_scalar(hot_row[:, r], tmp_a[:, r], -1.0, None, ALU.add).then_inc(s_dve, 1)
                step.n += 1
                step(dve.tensor_tensor(tmp_b[:, r], tok_f[:, r], below[:, r], ALU.subtract))
                step(dve.tensor_scalar(tmp_b[:, r], tmp_b[:, r], 0.0, float(NUM_COLD - 1), ALU.max, ALU.min))
                step(dve.tensor_scalar(tmp_a[:, r], hot_no[:, r], 0.0, SKIP, ALU.is_gt, ALU.mult))
                dve.tensor_tensor(cold_row[:, r], tmp_a[:, r], tmp_b[:, r], ALU.add).then_inc(s_rows, 1)

            def embed(c):
                s = c % 2
                dve.wait_ge(s_cvec, c + 1)
                dve.wait_ge(s_hotg[c % RING], 16 * (c // RING + 1))
                hv = hot_vec[c % RING]
                dve.tensor_tensor(hv[:, :], hv[:, :], bank(7 if s else 1), ALU.add).then_inc(s_h, 1)
                dve.wait_ge(s_h, c + 1)
                step(dve.bn_stats(stats[:, s, :], hv[:, :]))
                step(dve.bn_aggr(mv[:, s, :], stats[:, s, :]))
                dve.tensor_scalar(mv[:, s, 1:2], mv[:, s, 1:2], LN_EPS, None, ALU.add).then_inc(s_var, 1)

            def norm(c):
                s = c % 2
                dve.wait_ge(s_rstd, c + 1)
                if c >= 2:
                    dve.wait_ge(s_xT, c - 1)
                dve.tensor_scalar(xn[:, s, :], hot_vec[c % RING][:, :], mv[:, s, 0:1], rstd[:, s:s + 1],
                                  ALU.subtract, ALU.mult).then_inc(s_xn, 1)

            for k in range(BATCHES):
                for c in range(k * PER, (k + 1) * PER):
                    look_up(c)
                row_numbers(k)
            for c in range(NT + 1):
                if c < NT:
                    embed(c)
                if c >= 1:
                    norm(c - 1)
            att_dve(dve)
            moe_dve(dve)

        @block.tensor
        def _(pe):
            pe.wait_ge(s_const, 9)
            for c in range(HOT_C):
                pe.wait_ge(s_ohlo, c + 1)
                pe.wait_ge(s_chunk, c + 1)
                pe.wait_ge(s_row, c + 1)
                pe.matmul(bank(0)[0:HI, :], oh_hi[:, c, :], oh_lo[:, c, :, :].rearrange("p a n -> p (a n)"),
                          start=(c == 0), stop=False, skip_group_check=True)
                mm = pe.matmul(bank(0)[0:HI, 256:512], oh_hi_row[:, c, :], oh_lo[:, c, 0, :],
                               start=False, stop=(c == HOT_C - 1), skip_group_check=True)
            mm.then_inc(s_table, 1)
            for k in range(2):
                pe.wait_ge(s_toh, 8 * k + 8)
                for c in range(8):
                    mm = pe.transpose(bank(2 + k).bitcast(BF16)[0:HI, c * P:(c + 1) * P], tok_oh[:, 8 * k + c, :],
                                      ident_bf[:, :])
                mm.then_inc(s_tohT, 1)
            pe.wait_ge(s_seen, 1)
            pe.matmul(bank(1)[0:HI, 0:1], tri_bf[0:HI, 0:HI], seen_b[:, :], start=True,
                      stop=True).then_inc(s_base, 1)
            pe.wait_ge(s_tab, 1)
            pe.wait_ge(s_tohC, 2)
            for c in range(NT):
                if c >= 2:
                    pe.wait_ge(s_looked, 2 * (c - 1))
                b = bank(4 + c % 2)
                oh = tok_ohT[:, c, :]
                pe.matmul(b, oh, tab_a[:, :], start=True, stop=False, skip_group_check=True)
                pe.matmul(b[:, 256:512], oh, tab_b[:, :], start=False, stop=False, skip_group_check=True)
                pe.matmul(b[:, 0:1], oh, tab_c[:, :], start=False, stop=True,
                          skip_group_check=True).then_inc(s_look, 1)
            pe.wait_ge(s_proj, 16)
            for c in range(NT + 3):
                if c < NT:
                    pe.wait_ge(s_coldg[c % RING], 16 * (c // RING + 1))
                    if c >= 2:
                        pe.wait_ge(s_coldC, c - 1)
                    pe.transpose(bank(6 if c % 2 else 0)[:, 0:P], cold_lat[c % RING][:, :],
                                 ident[:, :]).then_inc(s_coldT, 1)
                if 1 <= c <= NT:
                    t = c - 1
                    pe.wait_ge(s_coldC, t + 1)
                    if t >= 2:
                        pe.wait_ge(s_h, t - 1)
                    pe.matmul(bank(7 if t % 2 else 1), cold_T[:, t % 2, :], projT[:, :], start=True,
                              stop=True).then_inc(s_cvec, 1)
                if c >= 3:
                    t = c - 3
                    pe.wait_ge(s_xn, t + 1)
                    if t >= 2:
                        pe.wait_ge(s_xC, t - 1)
                    for k in range(KC):
                        mm = pe.transpose(bank(2 + t % 2)[:, k * P:(k + 1) * P], xn[:, t % 2, k * P:(k + 1) * P],
                                          ident[:, :])
                    mm.then_inc(s_xT, 1)
            pe.wait_ge(s_xC, NT)
            att_pe(pe)
            moe_pe(pe)


def layouts(f):
    import numpy as np

    c = np.ascontiguousarray

    def gate_up(wg, wu):
        return c(np.concatenate([wg, wu], -1).reshape(-1, KC, P, D).transpose(0, 2, 1, 3))

    def down(wd):
        return c(wd.reshape(-1, FF // P, P, D).transpose(0, 2, 1, 3))

    return {
        "tok_ids": c(f["x"].reshape(NT, P).T),
        "hot_ids": c(f["L0_tok_hot_token_ids"].reshape(HOT_P, HOT_C)),
        "hot_emb": c(f["L0_tok_hot_emb_w"]),
        "cold_emb": c(f["L0_tok_cold_emb_w"]),
        "projT": c(f["L0_tok_proj_w"].T),
        "wqkv": c(f["L0_attn_w_project"].reshape(3, GROUPS, P, KC, P).transpose(1, 4, 3, 0, 2)
                  .reshape(GROUPS, P, KC, 3 * P)),
        "woT": c(f["L0_attn_w_out"].T.reshape(KC, P, D).transpose(1, 0, 2)),
        "wrT": c(f["L0_ffn_Wr"].T.reshape(KC, P, E).transpose(1, 0, 2)),
        "bias": c(np.broadcast_to(f["L0_ffn_bias"], (P, E))),
        "wgu": gate_up(f["L0_ffn_Wg"], f["L0_ffn_Wu"]),
        "wd": down(f["L0_ffn_Wd"]),
        "sgu": gate_up(f["L0_ffn_sWg"], f["L0_ffn_sWu"])[0],
        "sd": down(f["L0_ffn_sWd"])[0],
    }


def kernel(**inputs):
    import numpy as np
    import concourse.bacc as bacc
    from concourse.bass_utils import run_bass_kernel_spmd

    nc = bacc.Bacc("TRN2", target_bir_lowering=False, num_devices=1)
    arrays, aps = {}, {}
    for name, x in layouts({k: np.asarray(v) for k, v in inputs.items()}).items():
        arrays[f"in_{name}"] = x
        aps[name] = nc.dram_tensor(f"in_{name}", x.shape, mybir.dt.from_np(x.dtype), kind="ExternalInput").ap()
    out = nc.dram_tensor("out_0", (T + P, D), F32, kind="ExternalOutput").ap()
    build(nc, aps, out)
    r = run_bass_kernel_spmd(nc, [arrays], core_ids=[0])
    return r.results[0]["out_0"][:T].reshape(BATCH, SEQ, D)
```

```python
from contextlib import ExitStack

import concourse.bass as bass
from concourse import mybir

F32 = mybir.dt.float32
F32R = mybir.dt.float32r
BF16 = mybir.dt.bfloat16
I32 = mybir.dt.int32
U32 = mybir.dt.uint32
ALU = mybir.AluOpType
ACT = mybir.ActivationFunctionType
AX = mybir.AxisListType

P = 128
VOCAB, NUM_HOT, NUM_COLD = 32000, 8000, 24000
BATCH, SEQ, D = 2, 1024, 512
T = BATCH * SEQ
NT = T // P
KC = D // P
LATENT = 128
HEADS, HD = 16, 32
GROUPS, GH = HEADS // 4, 4
ATT_SCALE = float(HD) ** -0.5
QT = SEQ // P
LN_EPS = 1e-5
E, TOPK, FF = 16, 2, 256
W_EPS = 1e-9
HI = VOCAB // 256
HOT_P, HOT_C = 125, 64
SKIP = 100000.0
TILES = TOPK * T // P + E - 1
WRING = 4
LAG = 4
FILL0 = NT // BATCH + 3
FILL_STEP0, FILL_STEPS = 2, 5
PSLOTS = 2
SPLIT0 = 5
SLOT0 = 6
SLOT_RING = 6


class Chain:

    def __init__(self, eng, sem, start=0):
        self.eng, self.sem, self.n = eng, sem, start

    def __call__(self, ins):
        ins.then_inc(self.sem, 1)
        self.n = self.n + 1
        self.eng.wait_ge(self.sem, self.n)


def build(nc, a, out):
    ctx = ExitStack()
    with ctx:
        def sb(name, shape, dt=F32, where=ctx):
            return where.enter_context(nc.sbuf_tensor(name, shape, dt))

        def sem(name):
            return ctx.enter_context(nc.semaphore(name))

        ident = sb("ident", [P, P])
        ident_bf = sb("ident_bf", [P, P], BF16)
        tri_bf = sb("tri_bf", [P, P], BF16)
        ones_bf = sb("ones_bf", [P, P], BF16)
        mask_bf = sb("mask_bf", [P, P], BF16)
        iota_bf = sb("iota_bf", [P, 256], BF16)
        half_neg = sb("half_neg", [P, 1])
        iota_e = sb("iota_e", [P, E])
        iota_p128 = sb("iota_p128", [P, T // P])
        iota_j = sb("iota_j", [P, TILES])
        iota_f = sb("iota_f", [P, P])
        tok_no1 = sb("tok_no1", [P, NT])
        upto_e = sb("upto_e", [P, E, E])

        psum = ctx.enter_context(nc.psum_tensor("psum", [P, 8, 512], F32))

        def bank(i, n=1):
            return psum[:, i:i + n, :].rearrange("p a n -> p (a n)")

        xn2_dram = nc.dram_tensor("xn2_scratch", [T, D], F32, kind="Internal").ap()
        h_dram = nc.dram_tensor("h_scratch", [T, D], F32, kind="Internal").ap()

        xnT = sb("xnT", [P, KC, T])

        tok_ctx = ExitStack()
        tk = lambda name, shape, dt=F32: sb(name, shape, dt, tok_ctx)
        oh_hi = tk("oh_hi", [HOT_P, HOT_C, HI], BF16)
        oh_hi_row = tk("oh_hi_row", [HOT_P, HOT_C, HI], BF16)
        oh_lo = tk("oh_lo", [HOT_P, HOT_C, 2, 256], BF16)
        hot_ids = tk("hot_ids", [HOT_P, HOT_C], I32)
        tok_ids = tk("tok_ids", [P, NT], I32)
        hot_f = tk("hot_f", [HOT_P, HOT_C])
        hot_wrap = tk("hot_wrap", [HOT_P, HOT_C])
        hot_hi = tk("hot_hi", [HOT_P, HOT_C])
        hot_lo = tk("hot_lo", [HOT_P, HOT_C])
        hot_i = tk("hot_i", [HOT_P, 2, HOT_C], I32)
        row64 = tk("row64", [HOT_P, 1])
        chunk1 = tk("chunk1", [HOT_P, HOT_C])
        tok_f = tk("tok_f", [P, NT])
        tok_wrap = tk("tok_wrap", [P, NT])
        tok_i = tk("tok_i", [P, 3, NT], I32)
        tok_hi = tk("tok_hi", [P, NT])
        tok_lo = tk("tok_lo", [P, NT])
        seen = tk("seen", [HI, 256])
        seen_n = tk("seen_n", [HI, 1])
        seen_b = tk("seen_b", [HI, 1], BF16)
        rank_i = tk("rank_i", [HI, 3, 256], I32)
        tab_a = tk("tab_a", [HI, 512], BF16)
        tab_b = tk("tab_b", [HI, 256], BF16)
        tab_c = tk("tab_c", [HI, 1], BF16)
        tok_oh = tk("tok_oh", [P, NT, HI], BF16)
        tok_ohT = tk("tok_ohT", [HI, NT, P], BF16)
        prod = tk("prod", [P, 2, 2, 256])
        below = tk("below", [P, NT])
        hot_no = tk("hot_no", [P, NT])
        tmp_a = tk("tmp_a", [P, NT])
        tmp_b = tk("tmp_b", [P, NT])
        hot_row = tk("hot_row", [P, NT], I32)
        cold_row = tk("cold_row", [P, NT], I32)
        projT = tk("projT", [LATENT, D])
        hot_vec = [tk(f"hot_vec{i}", [P, D]) for i in range(NT)]
        cold_lat = [tk(f"cold_lat{i}", [P, LATENT]) for i in range(NT)]
        cold_T = tk("cold_T", [P, 2, P])
        stats = tk("stats", [P, 2, 6])
        mv = tk("mv", [P, 2, 2])
        rstd = tk("rstd", [P, 2])
        xn = tk("xn", [P, 2, D])
        tok_ctx.close()

        attnT = sb("attnT", [P, GROUPS * T])
        att_ctx = ExitStack()
        ak = lambda name, shape, dt=F32: sb(name, shape, dt, att_ctx)
        w_unit = ak("w_unit", [P, KC, 3 * P])
        full = ak("full", [P, 2, 512])
        part_hi = ak("part_hi", [P, 2, SEQ], F32R)
        part_lo = ak("part_lo", [P, 2, SEQ], F32R)
        q_stack, k_stack, v_unit = [], [], []
        for b in range(BATCH):
            v_unit.append(ak(f"v_unit{b}", [P, QT, P]))
            q_stack.append(ak(f"q_stack{b}", [P, GH, SEQ], F32R))
            k_stack.append(ak(f"k_stack{b}", [P, GH, SEQ], F32R))
        nmax = ak("nmax", [P, 4])
        probs = [ak(f"probs{i}", [P, SEQ]) for i in range(PSLOTS)]
        probsT = [ak("probsT0", [P, GH, SEQ - P]), ak("probsT1", [P, GH, SEQ])]
        z_sum = ak("z_sum", [P, 2, GH])
        z_rec = ak("z_rec", [P, 2, GH])
        z_inv = ak("z_inv", [P, 2, GH, HD])
        z_rows = ak("z_rows", [P, 2, P])
        att_ctx.close()

        acc = sb("acc", [P, NT, D])
        op_ctx = ExitStack()
        wo_hi = sb("wo_hi", [P, KC, D], F32R, op_ctx)
        wo_lo = sb("wo_lo", [P, KC, D], F32R, op_ctx)
        at_hi = sb("at_hi", [P, 2, D], F32R, op_ctx)
        at_lo = sb("at_lo", [P, 2, D], F32R, op_ctx)
        op_ctx.close()
        wo = acc[:, NT - KC:NT, :]
        rows_no = [sb(f"rows_no{i}", [P, 1], I32) for i in range(2)]
        x_rows = [sb(f"x_rows{i}", [P, D]) for i in range(2)]
        x_T = sb("x_T", [P, 2, D])
        silu_g = sb("silu_g", [P, 2, FF])
        gated = sb("gated", [P, 2, FF])
        gated_T = sb("gated_T", [P, 2, FF])
        y_sb = sb("y_sb", [P, 2, D])
        slot_lo = sb("slot_lo", [P, SLOT_RING, P])
        cmp_j = sb("cmp_j", [P, TILES, E])
        cmp_e = sb("cmp_e", [P, E, E])
        wr = sb("wr", [P, KC, E])
        bias = sb("bias", [P, E])
        xn2 = sb("xn2", [P, 2, D])
        stats2 = sb("stats2", [P, 2, 6])
        mv2 = sb("mv2", [P, 2, 2])
        rstd2 = sb("rstd2", [P, 2])
        ws_hi = sb("ws_hi", [P, KC + 2, D], F32R)
        ws_lo = sb("ws_lo", [P, KC + 2, D], F32R)
        w_dn = sb("w_dn", [P, WRING, 2, D])
        ws_full = w_dn[:, :, :, :].rearrange("p s k n -> p (s k) n")
        xs_hi = sb("xs_hi", [P, 2, D], F32R)
        xs_lo = sb("xs_lo", [P, 2, D], F32R)
        gs_hi = sb("gs_hi", [P, 2, FF], F32R)
        gs_lo = sb("gs_lo", [P, 2, FF], F32R)
        logits = sb("logits", [P, NT, E])
        row_red = sb("row_red", [P, NT])
        probs_e = sb("probs_e", [P, NT, E])
        top_v = sb("top_v", [P, NT, 8])
        top_i = sb("top_i", [P, NT, 8], U32)
        top_f = sb("top_f", [P, NT, TOPK])
        w_sum = sb("w_sum", [P, NT])
        w_top = sb("w_top", [P, NT, TOPK])
        oh_e = sb("oh_e", [P, TOPK, NT, E])
        oh_any = sb("oh_any", [P, NT, E], BF16)
        count_e = sb("count_e", [P, E])
        tiles_e = sb("tiles_e", [P, E])
        tiles_to = sb("tiles_to", [P, E])
        tiles_to_i = sb("tiles_to_i", [P, E], I32)
        base_e = sb("base_e", [P, E])
        pos_all = sb("pos_all", [P, NT, E])
        pos_pick = sb("pos_pick", [P, NT, E])
        pos_f = sb("pos_f", [P, TOPK, NT])
        pos_i = sb("pos_i", [P, TOPK, NT], I32)
        pos_hl = sb("pos_hl", [P, 2, TOPK, NT], I32)
        pos_hlf = sb("pos_hlf", [P, 2, TOPK, NT])
        tile_e = sb("tile_e", [P, TILES])
        tile_e_i = sb("tile_e_i", [P, TILES], I32)
        slot_hi = sb("slot_hi", [P, SLOT_RING, 2, TILES])
        slot_f = sb("slot_f", [P, TILES])
        slot_tok = sb("slot_tok", [P, TILES], I32)
        slot_w = sb("slot_w", [P, TILES])
        slot_pad = sb("slot_pad", [P, TILES])
        slot_out = sb("slot_out", [P, TILES], I32)
        pad_row = sb("pad_row", [P, 1])
        out_no = [sb(f"out_no{i}", [P, 1], I32) for i in range(2)]

        w_gu = attnT[:, :].rearrange("p (s k n) -> p s k n", s=WRING, k=KC)

        s_dve2 = sem("dve_router_step")
        s_passed = sem("pool_waits_passed")
        s_moec = sem("router_constants_ready")
        s_wo = sem("output_weights_loaded")
        s_wohi = sem("output_weights_high_ready")
        s_wolo = sem("output_weights_low_ready")
        s_athi = sem("attention_tile_high_ready")
        s_atlo = sem("attention_tile_low_ready")
        s_rtw = sem("router_weights_loaded")
        s_hl = [sem(f"h_loaded{i}") for i in range(NT)]
        s_sw = sem("shared_weights_loaded")
        s_wshi = sem("shared_weights_high_ready")
        s_wslo = sem("shared_weights_low_ready")
        s_xshi = sem("shared_rows_high_ready")
        s_xslo = sem("shared_rows_low_ready")
        s_gshi = sem("shared_gated_high_ready")
        s_op = sem("output_projected")
        s_acc = sem("residual_ready")
        s_var2 = sem("variance2_ready")
        s_rstd2 = sem("rstd2_ready")
        s_xn2 = sem("xn2_ready")
        s_xst = [sem(f"xn2_stored{i}") for i in range(2)]
        s_x2T = sem("xn2_turned")
        s_x2C = sem("xn2T_ready")
        s_lg = sem("logits_summed")
        s_lgc = sem("logits_copied")
        s_shift = sem("logits_shifted")
        s_exp = sem("router_exp_ready")
        s_oh = sem("choices_ready")
        s_rank = sem("ranks_summed")
        s_slot = sem("slot_onehots_ready")
        s_slotm = sem("slot_matmuls_done")
        s_plan = sem("plan_ready")
        s_gu = sem("gate_up_ready")
        s_silu = sem("silu_ready")
        s_gated = sem("gated_ready")
        s_gT = sem("gated_turned")
        s_gC = sem("gated_T_ready")
        s_y = sem("down_ready")
        s_yc = sem("y_copied")
        s_rn = sem("row_numbers_copied")
        s_xg = [sem(f"rows_gathered{i}") for i in range(2)]
        s_xT2 = sem("rows_turned")
        s_xC2 = sem("rows_T_ready")
        s_wl = [sem(f"expert_loaded{i}") for i in range(WRING)]
        s_wr = sem("expert_weights_ready")
        s_on = sem("out_row_numbers_copied")
        s_yadd = sem("y_added")
        s_pad = sem("spare_rows_stored")
        s_out = sem("out_stored")
        s_w = sem("unit_weights_loaded")
        s_fill = sem("projection_ready")
        s_fact = sem("projection_copied_by_act")
        s_fdve = sem("projection_copied_by_dve")
        s_hi = sem("high_parts_ready")
        s_lo = sem("low_parts_ready")
        s_stack = [sem(f"stacks_loaded{b}") for b in range(BATCH)]
        s_S = sem("scores_ready")
        s_M = sem("row_max_ready")
        s_E = sem("probs_ready")
        s_T = sem("probs_turned")
        s_Ca = sem("probsT_copied_by_act")
        s_Cd = sem("probsT_copied_by_dve")
        s_Zr = sem("z_reciprocal_ready")
        s_Z = sem("z_inverse_ready")
        s_PV = sem("heads_summed")
        s_ZR = sem("z_rows_ready")
        s_AT = sem("attnT_ready")
        s_in = sem("ids_loaded")
        s_proj = sem("projT_loaded")
        s_const = sem("constants_ready")
        s_pool = sem("pool_step")
        s_dve = sem("dve_step")
        s_ohhi = sem("hot_onehot_hi_ready")
        s_ohlo = sem("hot_onehot_lo_ready")
        s_row = sem("hot_row_part_ready")
        s_chunk = sem("even_chunk_part_ready")
        s_chunk_act = sem("odd_chunk_part_ready")
        s_table = sem("table_summed")
        s_seen = sem("seen_counted")
        s_zero = sem("gather_buffers_zeroed")
        s_base = sem("base_summed")
        s_tab = sem("tables_ready")
        s_toh = sem("token_onehot_ready")
        s_tohT = sem("token_onehot_turned")
        s_tohC = sem("token_onehot_copied")
        s_look = sem("lookup_multiplied")
        s_looked = sem("lookup_reduced")
        s_rows = sem("row_numbers_ready")
        s_hotg = [sem(f"hot_gathered{i}") for i in range(NT)]
        s_coldg = [sem(f"cold_gathered{i}") for i in range(NT)]
        s_coldT = sem("cold_turned")
        s_coldC = sem("cold_copied")
        s_cvec = sem("cold_projected")
        s_h = sem("h_ready")
        s_hst = sem("h_stored")
        s_var = sem("variance_ready")
        s_rstd = sem("rstd_ready")
        s_xn = sem("xn_ready")
        s_xT = sem("xn_turned")
        s_xC = sem("xnT_ready")
        block = ctx.enter_context(nc.Block())

        BATCHES = 4
        PER = NT // BATCHES

        HEAD = 16
        STACKED = 16 * 8 * GH
        STEPS = QT * GH
        FILLS = 6

        def turned_banks(i):
            return 1 if i < 4 else 2

        def copier(i, h, k):
            return "dve" if k else "act"

        banks = [(i, h, k) for i in range(QT) for h in range(GH) for k in range(turned_banks(i))]
        UB = len(banks)
        UCOPY = {e: sum(copier(*x) == e for x in banks) for e in ("act", "dve")}

        def bank_no(i, h, k):
            return banks.index((i, h, k))

        def copies(e, upto):
            return sum(copier(*x) == e for x in banks[:upto])

        def wait_bank_free(pe, u, n):
            m = n - 2
            x = banks[m % UB]
            v = u if m >= 0 else u - 1
            e = copier(*x)
            pe.wait_ge(s_Ca if e == "act" else s_Cd, HEAD + v * UCOPY[e] + copies(e, m % UB + 1))

        def load_w(sp, g):
            sp.dma_start(w_unit[:, :, :], a["wqkv"][g] if isinstance(g, int) else
                         a["wqkv"][bass.ds(g, 1), :, :, :].rearrange("o p k n -> (o p) k n")).then_inc(s_w, 16)

        def stack(sp, u, b, sides=(0, 1), first=False):
            if not first:
                sp.wait_ge(s_S, HEAD + (u - 1) * STEPS)
            for side in sides:
                st = (q_stack, k_stack)[side][b]
                sp.wait_ge(s_lo, HEAD + 4 * u + 2 * side + 2)
                for r in range(4):
                    low = r % 2 if side == 0 else r // 2
                    src = part_lo if low else part_hi
                    for h in range(GH):
                        sp.dma_start(st[32 * r:32 * r + 32, h, :].bitcast(F32),
                                     src[32 * h:32 * h + 32, side, :].bitcast(F32)).then_inc(s_stack[b], 16)

        def att_sp(sp):
            def group(g, last):
                stack(sp, 2 * g + 1, 1)
                if not last:
                    sp.wait_ge(s_fill, HEAD + 2 * FILLS * (g + 1))
                    load_w(sp, g + 1)
                    stack(sp, 2 * g + 2, 0)

            with sp.Fori(0, GROUPS - 1) as g:
                group(g, False)
            group(GROUPS - 1, True)

        def passed(pool):
            pool.sem_inc(s_passed, 1)

        def split_part(pool, u, b, side, half, loaded):
            c = slice(half * 512, half * 512 + 512)
            pool.wait_ge(s_fact if side == 0 else s_fdve, HEAD + 3 * u + half + 1)
            if loaded is not None:
                pool.wait_ge(s_stack[1 - b], loaded)
            passed(pool)
            pool.tensor_copy(part_hi[:, side, c], full[:, side, :]).then_inc(s_hi, 1)
            pool.wait_ge(s_hi, HEAD + 4 * u + 2 * side + half + 1)
            pool.tensor_tensor(part_lo[:, side, c], full[:, side, :],
                               part_hi[:, side, c].bitcast(F32), ALU.subtract).then_inc(s_lo, 1)

        def att_pool(pool):
            def split(u, b, loaded):
                for side in range(2):
                    for half in range(2):
                        split_part(pool, u, b, side, half, loaded)

            def group(g, last):
                split(2 * g + 1, 1, STACKED * (g + 1))
                if not last:
                    split(2 * g + 2, 0, STACKED * (g + 1))

            with pool.Fori(0, GROUPS - 1) as g:
                group(g, False)
            group(GROUPS - 1, True)

        def fill_evac(eng, who, u, f, b):
            src = bank(7)
            n = HEAD + FILLS * u + f + 1
            if f in (0, 1) and who == "act":
                eng.wait_ge(s_fill, n)
                eng.wait_ge(s_lo, HEAD + 4 * u + (f if f else -2))
                eng.activation(full[:, 0, :], src, ACT.Copy, scale=-ATT_SCALE).then_inc(s_fact, 1)
            if f in (2, 3) and who == "dve":
                eng.wait_ge(s_fill, n)
                eng.wait_ge(s_lo, HEAD + 4 * u + (3 if f == 3 else 0))
                eng.tensor_copy(full[:, 1, :], src).then_inc(s_fdve, 1)
            if f in (4, 5) and who == ("act", "dve")[f - 4]:
                eng.wait_ge(s_fill, n)
                eng.wait_ge(s_PV, HEAD + (u - 1) * QT)
                dst = v_unit[b][:, 4 * (f - 4):4 * (f - 4) + 4, :].rearrange("p a n -> p (a n)")
                if who == "act":
                    eng.copy(dst, src).then_inc(s_fact, 1)
                else:
                    eng.tensor_copy(dst, src).then_inc(s_fdve, 1)

        def fill_piece(pe, u, b, f, k, loads):
            if k == 0:
                pe.wait_ge(s_w, loads)
                copied, count = ((s_fdve, 0), (s_fact, 1), (s_fact, 2), (s_fdve, 1), (s_fdve, 2), (s_fact, 3))[f]
                pe.wait_ge(copied, HEAD + 3 * u + count)
            if f < 4:
                side, half = f // 2, f % 2
                t0 = b * SEQ + half * 512
                mm = pe.matmul(bank(7), w_unit[:, k, side * P:(side + 1) * P], xnT[:, k, t0:t0 + 512],
                               start=(k == 0), stop=(k == KC - 1), skip_group_check=True)
            else:
                t0 = b * SEQ + ((f - 4) * 4 + k) * P
                for c in range(KC):
                    mm = pe.matmul(bank(7)[:, k * P:(k + 1) * P], xnT[:, c, t0:t0 + P],
                                   w_unit[:, c, 2 * P:3 * P], start=(c == 0), stop=(c == KC - 1))
            if k == KC - 1:
                mm.then_inc(s_fill, 1)

        def att_pe(pe):
            def scores(u, b, n):
                i, h = n // GH, n % GH
                pe.wait_ge(s_E, HEAD + u * STEPS + n - 1)
                dst = bank(2 * (n % 2), 2)
                qs = q_stack[b][:, h, i * P:(i + 1) * P]
                for c0 in range(0, (i + 1) * P, 512):
                    c1 = min(max((i + 1) * P, c0 + 256), c0 + 512)
                    own = c0 <= i * P < c1
                    mm = pe.matmul(dst[:, c0:c1], qs, k_stack[b][:, h, c0:c1], start=True, stop=not own)
                    if own:
                        mm = pe.matmul(dst[:, i * P:(i + 1) * P], ident_bf[:, :], mask_bf[:, :], start=False,
                                       stop=True)
                mm.then_inc(s_S, 1)

            def turn(u, n):
                i, h = n // GH, n % GH
                pe.wait_ge(s_E, HEAD + u * STEPS + n + 1)
                for k in range(turned_banks(i)):
                    m = bank_no(i, h, k)
                    wait_bank_free(pe, u, m)
                    for j in range(4 * k, min(4 * k + 4, i + 1)):
                        mm = pe.transpose(bank(4 + m % 2)[:, (j - 4 * k) * P:(j - 4 * k + 1) * P],
                                          probs[n % PSLOTS][:, j * P:(j + 1) * P], ident[:, :])
                    mm.then_inc(s_T, 1)

            def heads(u, b, i):
                last = bank_no(i, GH - 1, turned_banks(i) - 1) + 1
                for e, s in (("act", s_Ca), ("dve", s_Cd)):
                    pe.wait_ge(s, HEAD + u * UCOPY[e] + copies(e, last))
                pe.wait_ge(s_AT, HEAD + u * QT + i)
                for j in range(i + 1):
                    for h in range(GH):
                        pe.matmul(bank(6)[32 * h:32 * h + 32, 0:P], v_unit[b][:, j, 32 * h:32 * h + 32],
                                  probsT[i % 2][:, h, j * P:(j + 1) * P], start=(j == 0), stop=(j == i))
                pe.wait_ge(s_Z, HEAD + u * QT + i + 1)
                pe.transpose(bank(6)[:, P:2 * P], z_inv[:, i % 2, :, :].rearrange("p h d -> p (h d)"),
                             ident[:, :]).then_inc(s_PV, 1)

            def unit(u, b, g, prev, nxt):
                for n in range(STEPS):
                    if n + 1 < STEPS:
                        scores(u, b, n + 1)
                    elif nxt:
                        first_scores(u + 1, 1 - b, g + b)
                    if n >= 1:
                        turn(u, n - 1)
                    elif prev:
                        turn(u - 1, STEPS - 1)
                    f, k = divmod(n - FILL_STEP0, FILL_STEPS)
                    if nxt and 0 <= f < FILLS and k < KC:
                        fill_piece(pe, u + 1, 1 - b, f, k, 16 * (g + 1 + b))
                    if n % GH == 2:
                        if n > GH:
                            heads(u, b, n // GH - 1)
                        elif prev:
                            heads(u - 1, 1 - b, QT - 1)

            def first_scores(u, b, g):
                pe.wait_ge(s_stack[b], STACKED * (g + 1))
                pe.wait_ge(s_fact, HEAD + 3 * u + 3)
                pe.wait_ge(s_fdve, HEAD + 3 * u + 3)
                scores(u, b, 0)

            first_scores(0, 0, 0)
            unit(0, 0, 0, False, True)
            with pe.Fori(0, GROUPS - 1) as g:
                unit(2 * g + 1, 1, g, True, True)
                unit(2 * g + 2, 0, g + 1, True, True)
            last = 2 * GROUPS - 1
            unit(last, 1, GROUPS - 1, True, False)
            turn(last, STEPS - 1)
            heads(last, 1, QT - 1)

        def copy_turned(eng, who, u, n):
            i, h = n // GH, n % GH
            for k in range(turned_banks(i)):
                if copier(i, h, k) != who:
                    continue
                m = bank_no(i, h, k)
                eng.wait_ge(s_T, HEAD + u * UB + m + 1)
                eng.wait_ge(s_PV, HEAD + u * QT + i - 1)
                c0, c1 = 4 * k * P, min(4 * k + 4, i + 1) * P
                dst, src = probsT[i % 2][:, h, c0:c1], bank(4 + m % 2)[:, 0:c1 - c0]
                if who == "act":
                    eng.copy(dst, src).then_inc(s_Ca, 1)
                else:
                    eng.tensor_copy(dst, src).then_inc(s_Cd, 1)

        def att_act(act):
            def exp(u, n):
                i, h = n // GH, n % GH
                act.wait_ge(s_M, HEAD + u * STEPS + n + 1)
                if n >= 2:
                    j, k = (n - 2) // GH, (n - 2) % GH
                    act.wait_ge(s_T, HEAD + u * UB + bank_no(j, k, turned_banks(j) - 1) + 1)
                else:
                    act.wait_ge(s_T, HEAD + u * UB - (2 if n == 0 else 0))
                act.wait_ge(s_Z, HEAD + u * QT + i - 1)
                act.activation(probs[n % PSLOTS][:, 0:(i + 1) * P], bank(2 * (n % 2), 2)[:, 0:(i + 1) * P], ACT.Exp,
                               bias=nmax[:, n % 4:n % 4 + 1], scale=-1.0,
                               accum_out=z_sum[:, i % 2, h:h + 1]).then_inc(s_E, 1)

            def z_row(u, i):
                act.wait_ge(s_PV, HEAD + u * QT + i + 1)
                act.wait_ge(s_AT, HEAD + u * QT + i - 1)
                act.copy(z_rows[:, i % 2, :], bank(6)[:, P:2 * P]).then_inc(s_ZR, 1)

            def unit(u, b, prev, nxt):
                for n in range(STEPS):
                    if n >= 2:
                        copy_turned(act, "act", u, n - 2)
                    elif prev:
                        copy_turned(act, "act", u - 1, STEPS + n - 2)
                    exp(u, n)
                    f, k = divmod(n - FILL_STEP0, FILL_STEPS)
                    if nxt and 0 <= f < FILLS and k == KC:
                        fill_evac(act, "act", u + 1, f, 1 - b)
                    if n % GH == 3:
                        if n > GH:
                            z_row(u, n // GH - 1)
                        elif prev:
                            z_row(u - 1, QT - 1)

            unit(0, 0, False, True)
            with act.Fori(0, GROUPS - 1) as g:
                unit(2 * g + 1, 1, True, True)
                unit(2 * g + 2, 0, True, True)
            last = 2 * GROUPS - 1
            unit(last, 1, True, False)
            for n in (STEPS - 2, STEPS - 1):
                copy_turned(act, "act", last, n)
            z_row(last, QT - 1)

        def att_dve(dve):
            def row_max(u, n):
                i = n // GH
                dve.wait_ge(s_S, HEAD + u * STEPS + n + 1)
                dve.wait_ge(s_E, HEAD + u * STEPS + n - 3)
                dve.tensor_reduce(nmax[:, n % 4:n % 4 + 1], bank(2 * (n % 2), 2)[:, 0:(i + 1) * P], AX.X,
                                  ALU.min).then_inc(s_M, 1)

            def z_invert(u, i):
                dve.wait_ge(s_E, HEAD + u * STEPS + GH * i + GH)
                dve.wait_ge(s_PV, HEAD + u * QT + i - 1)
                dve.reciprocal(z_rec[:, i % 2, :], z_sum[:, i % 2, :]).then_inc(s_Zr, 1)
                dve.wait_ge(s_Zr, HEAD + u * QT + i + 1)
                dve.tensor_copy(z_inv[:, i % 2, :, :],
                                z_rec[:, i % 2, :].unsqueeze(2).to_broadcast([P, GH, HD])).then_inc(s_Z, 1)

            def normalize(u, b, i, g):
                dve.wait_ge(s_ZR, HEAD + u * QT + i + 1)
                dst = attnT[:, bass.ds(g * T + (b * SEQ + i * P), P)]
                dve.tensor_tensor(dst, bank(6)[:, 0:P], z_rows[:, i % 2, :], ALU.mult).then_inc(s_AT, 1)

            def unit(u, b, g, pg, nxt):
                for n in range(STEPS):
                    row_max(u, n)
                    f, k = divmod(n - FILL_STEP0, FILL_STEPS)
                    if nxt and 0 <= f < FILLS and k == KC:
                        fill_evac(dve, "dve", u + 1, f, 1 - b)
                    if n >= 2:
                        copy_turned(dve, "dve", u, n - 2)
                    elif pg is not None:
                        copy_turned(dve, "dve", u - 1, STEPS + n - 2)
                    if n % GH == 0:
                        if n:
                            z_invert(u, n // GH - 1)
                        elif pg is not None:
                            z_invert(u - 1, QT - 1)
                    if n % GH == 3:
                        if n > GH:
                            normalize(u, b, n // GH - 1, g)
                        elif pg is not None:
                            normalize(u - 1, 1 - b, QT - 1, pg)

            unit(0, 0, 0, None, True)
            with dve.Fori(0, GROUPS - 1) as g:
                unit(2 * g + 1, 1, g, g, True)
                unit(2 * g + 2, 0, g + 1, g, True)
            last = 2 * GROUPS - 1
            unit(last, 1, GROUPS - 1, GROUPS - 1, False)
            for n in (STEPS - 2, STEPS - 1):
                copy_turned(dve, "dve", last, n)
            z_invert(last, QT - 1)
            normalize(last, 1, QT - 1, GROUPS - 1)

        def inv_std(pool, c):
            pool.wait_ge(s_var, c + 1)
            if c >= 2:
                pool.wait_ge(s_xn, c - 1)
            pool.tensor_tensor(rstd[:, c % 2:c % 2 + 1], mv[:, c % 2, 1:2], half_neg[:, :],
                               ALU.pow).then_inc(s_rstd, 1)

        ATT_DONE = HEAD + 2 * GROUPS * QT
        LAST = TILES - 1
        SHARED = NT
        PLANNED = 5


        def attn_tile(c):
            return attnT[:, :].rearrange("p (g t) -> p g t", g=GROUPS)[:, :, c * P:(c + 1) * P]

        def moe_sp(sp):
            units = 2 * GROUPS
            sp.wait_ge(s_hst, 16 * NT)
            sp.wait_ge(s_fill, HEAD + FILLS * units)
            sp.wait_ge(s_stack[1], STACKED * GROUPS)
            sp.wait_ge(s_fact, HEAD + FILLS // 2 * units)
            sp.wait_ge(s_fdve, HEAD + FILLS // 2 * units)
            sp.wait_ge(s_S, HEAD + STEPS * (units - 1))
            sp.wait_ge(s_PV, HEAD + QT * (units - 1))
            sp.dma_start(wo[:, :, :], a["woT"]).then_inc(s_wo, 16)
            for c in range(NT):
                if c == NT - KC:
                    sp.wait_ge(s_wolo, KC)
                sp.dma_start(acc[:, c, :], h_dram[c * P:(c + 1) * P, :]).then_inc(s_hl[c], 16)
            sp.dma_start(wr[:, :, :], a["wrT"]).then_inc(s_rtw, 16)
            sp.dma_start(bias[:, :], a["bias"]).then_inc(s_rtw, 16)
            sp.wait_ge(s_AT, ATT_DONE)
            sp.dma_start(ws_full[:, 0:KC, :], a["sgu"]).then_inc(s_sw, 16)
            sp.dma_start(ws_full[:, KC:KC + 2, :], a["sd"]).then_inc(s_sw, 16)
            for c in range(NT):
                sp.wait_ge(s_xn2, c + 1)
                sp.dma_start(xn2_dram[c * P:(c + 1) * P, :], xn2[:, c % 2, :]).then_inc(s_xst[c % 2], 16)

            def load(e, s):
                src_gu = a["wgu"][bass.ds(e, 1), :, :, :].rearrange("o p k n -> (o p) k n")
                src_dn = a["wd"][bass.ds(e, 1), :, :, :].rearrange("o p k n -> (o p) k n")
                sp.dma_start(w_gu[:, s, :, :], src_gu).then_inc(s_wl[s], 16)
                sp.dma_start(w_dn[:, s, :, :], src_dn).then_inc(s_wl[s], 16)

            def ready(m, s):
                sp.wait_ge(s_wl[s], 32 * (m + 1))
                sp.sem_inc(s_wr, 1)

            def store(c):
                sp.wait_ge(s_acc, c + 1)
                sp.dma_start(out[c * P:(c + 1) * P, :], acc[:, c, :]).then_inc(s_out, 16)

            sp.wait_ge(s_op, NT)
            sp.wait_ge(s_wslo, NT)
            for s in range(WRING):
                load(s, s)
            for s in range(WRING):
                ready(0, s)
            for c in range(NT):
                store(c)
            sp.dma_start(out[T:T + P, :], acc[:, 0, :]).then_inc(s_pad, 16)
            sp.wait_ge(s_plan, PLANNED)
            with sp.Fori(1, E // WRING) as m:
                for s in range(WRING):
                    done = sp.value_load(tiles_to_i[0:1, bass.ds(WRING * m + (s - WRING), 1)], min_val=0,
                                         max_val=TILES)
                    sp.wait_ge(s_y, done + SHARED)
                    load(WRING * m + s, s)
                    ready(m, s)
            sp.wait_ge(s_yadd, 16 * TILES)

        def moe_pool(pool):
            pool.wait_ge(s_wo, 16)
            for k in range(KC):
                pool.tensor_copy(wo_hi[:, k, :], wo[:, k, :]).then_inc(s_wohi, 1)
                pool.wait_ge(s_wohi, k + 1)
                pool.tensor_tensor(wo_lo[:, k, :], wo[:, k, :], wo_hi[:, k, :].bitcast(F32),
                                   ALU.subtract).then_inc(s_wolo, 1)

            def split_weights(c):
                w = (KC + 2) * D // NT
                part = lambda x: x.rearrange("p k n -> p (k n)")[:, c * w:(c + 1) * w]
                if c == 0:
                    pool.wait_ge(s_sw, 32)
                pool.tensor_copy(part(ws_hi[:, :, :]), part(ws_full[:, 0:KC + 2, :])).then_inc(s_wshi, 1)
                pool.wait_ge(s_wshi, c + 1)
                pool.tensor_tensor(part(ws_lo[:, :, :]), part(ws_full[:, 0:KC + 2, :]),
                                   part(ws_hi[:, :, :]).bitcast(F32), ALU.subtract).then_inc(s_wslo, 1)

            def split_rows(c):
                s = c % 2
                src = xnT[:, :, c * P:(c + 1) * P]
                pool.wait_ge(s_x2C, c + 1)
                if c >= 2:
                    pool.wait_ge(s_gu, c - 1)
                hi = xs_hi[:, s, :].rearrange("p (k n) -> p k n", k=KC)
                lo = xs_lo[:, s, :].rearrange("p (k n) -> p k n", k=KC)
                pool.tensor_copy(hi, src).then_inc(s_xshi, 1)
                pool.wait_ge(s_xshi, c + 1)
                pool.tensor_tensor(lo, src, hi.bitcast(F32), ALU.subtract).then_inc(s_xslo, 1)

            for c in range(NT):
                pool.wait_ge(s_var2, c + 1)
                if c >= 2:
                    pool.wait_ge(s_xn2, c - 1)
                pool.tensor_tensor(rstd2[:, c % 2:c % 2 + 1], mv2[:, c % 2, 1:2], half_neg[:, :],
                                   ALU.pow).then_inc(s_rstd2, 1)
                if 0 <= c - SPLIT0 < NT // 2:
                    split_weights(2 * (c - SPLIT0))
                    split_weights(2 * (c - SPLIT0) + 1)
                if c in (NT - 3, NT - 2):
                    split_rows(c - NT + 3)
            for c in range(2, NT):
                split_rows(c)
            for s in range(2):
                pool.wait_ge(s_xst[s], 16 * (NT // 2))
            pool.wait_ge(s_plan, PLANNED)

            def gather(m, s, first):
                if not first:
                    pool.wait_ge(s_xT2, 2 * m + (s - 1))
                    pool.wait_ge(s_xg[s], 16 * m)
                    passed(pool)
                pool.tensor_copy(rows_no[s][:, :], slot_tok[:, bass.ds(2 * m + s, 1)]).then_inc(s_rn, 1)
                pool.wait_ge(s_rn, 2 * m + (s + 1))
                passed(pool)
                pool.indirect_dma_start(
                    out=x_rows[s][:, :], out_offset=None, in_=xn2_dram,
                    in_offset=bass.IndirectOffsetOnAxis(ap=rows_no[s][:, :], axis=0),
                    bounds_check=T - 1, oob_is_err=False).then_inc(s_xg[s], 16)

            def add(m, s, first):
                pool.wait_ge(s_yc, 2 * m + (s + 1))
                if not first:
                    pool.wait_ge(s_yadd, 16 * (2 * m + s))
                passed(pool)
                pool.tensor_copy(out_no[s][:, :], slot_out[:, bass.ds(2 * m + s, 1)]).then_inc(s_on, 1)
                pool.wait_ge(s_on, 2 * m + (s + 1))
                passed(pool)
                pool.indirect_dma_start(
                    out=out, out_offset=bass.IndirectOffsetOnAxis(ap=out_no[s][:, :], axis=0),
                    in_=y_sb[:, s, :], in_offset=None, bounds_check=T + P - 1, oob_is_err=True,
                    compute_op=ALU.add).then_inc(s_yadd, 16)

            gather(0, 0, True)
            gather(0, 1, True)
            gather(1, 0, False)
            gather(1, 1, False)
            pool.wait_ge(s_out, 16 * NT)
            pool.wait_ge(s_pad, 16)
            passed(pool)
            add(0, 0, True)
            with pool.Fori(2, TILES // 2) as m:
                gather(m, 0, False)
                add(m - 2, 1, False)
                gather(m, 1, False)
                add(m - 1, 0, False)
            gather(TILES // 2, 0, False)
            for j in range(TILES - 4, TILES):
                add(j // 2, j % 2, False)

        def moe_act(act):
            def router_exp(q):
                r = slice(q * (NT // 2), (q + 1) * (NT // 2))
                act.wait_ge(s_shift, q + 1)
                act.activation(probs_e[:, r, :], logits[:, r, :], ACT.Exp).then_inc(s_exp, 1)

            def attention_high(c):
                if c >= 2:
                    act.wait_ge(s_op, c - 1)
                act.copy(at_hi[:, c % 2, :].rearrange("p (g n) -> p g n", g=GROUPS),
                         attn_tile(c)).then_inc(s_athi, 1)

            act.wait_ge(s_AT, ATT_DONE)
            for c in range(4):
                attention_high(c)
            for c in range(NT):
                act.wait_ge(s_x2T, c + 1)
                act.copy(xnT[:, :, c * P:(c + 1) * P],
                         bank(2 + c % 2).rearrange("p (k n) -> p k n", k=KC)).then_inc(s_x2C, 1)
                if c + 4 < NT:
                    attention_high(c + 4)
                if c == NT // 2 + 2:
                    router_exp(0)
            router_exp(1)

            def silu(n, p):
                act.wait_ge(s_gu, n + 1)
                if not isinstance(n, int) or n >= 2:
                    act.wait_ge(s_gated, n - 1)
                act.activation(silu_g[:, p, :], bank(2 + p)[:, 0:FF], ACT.Silu).then_inc(s_silu, 1)

            def turn_copy(n, p):
                act.wait_ge(s_gT, n + 1)
                if not isinstance(n, int) or n >= 2:
                    act.wait_ge(s_y, n - 1)
                act.copy(gated_T[:, p, :], bank(4 + p)[:, 0:FF]).then_inc(s_gC, 1)

            def turn_high(n):
                act.wait_ge(s_gT, n + 1)
                if n >= 2:
                    act.wait_ge(s_y, n - 1)
                act.copy(gs_hi[:, n % 2, :], bank(4 + n % 2)[:, 0:FF]).then_inc(s_gshi, 1)

            for n in range(SHARED):
                if n >= 1:
                    turn_high(n - 1)
                silu(n, n % 2)

            def routed(m, s, first, added):
                n = SHARED + 2 * m + s
                q = 1 - s
                if first:
                    turn_high(n - 1)
                else:
                    turn_copy(n - 1, q)
                silu(n, s)
                if not first:
                    y_scale(n - 1, q, added)

            def y_scale(n, q, added):
                act.wait_ge(s_y, n + 1)
                if added is not None:
                    act.wait_ge(s_yadd, added)
                act.activation(y_sb[:, q, :], bank(6 + q), ACT.Copy,
                               scale=slot_w[:, bass.ds(n - SHARED, 1)]).then_inc(s_yc, 1)

            routed(0, 0, True, None)
            routed(0, 1, False, None)
            routed(1, 0, False, None)
            routed(1, 1, False, 16)
            with act.Fori(2, TILES // 2) as m:
                routed(m, 0, False, 16 * (2 * m - 2))
                routed(m, 1, False, 16 * (2 * m - 1))
            routed(TILES // 2, 0, False, 16 * (LAST - 2))
            turn_copy(SHARED + LAST, 0)
            y_scale(SHARED + LAST, 0, 16 * (LAST - 1))

        def moe_dve(dve):
            step = Chain(dve, s_dve2)

            def residual(c):
                s = c % 2
                dve.wait_ge(s_op, c + 1)
                dve.wait_ge(s_hl[c], 16)
                step(dve.tensor_tensor(acc[:, c, :], acc[:, c, :], bank(s), ALU.add))
                step(dve.bn_stats(stats2[:, s, :], acc[:, c, :]))
                step(dve.bn_aggr(mv2[:, s, :], stats2[:, s, :]))
                dve.tensor_scalar(mv2[:, s, 1:2], mv2[:, s, 1:2], LN_EPS, None, ALU.add).then_inc(s_var2, 1)

            def norm2(c):
                s = c % 2
                dve.wait_ge(s_rstd2, c + 1)
                if c >= 2:
                    dve.wait_ge(s_x2T, c - 1)
                    dve.wait_ge(s_xst[s], 16 * (c // 2))
                dve.tensor_scalar(xn2[:, s, :], acc[:, c, :], mv2[:, s, 0:1], rstd2[:, s:s + 1],
                                  ALU.subtract, ALU.mult).then_inc(s_xn2, 1)

            def logit(c):
                dve.wait_ge(s_lg, c + 1)
                if c == 0:
                    dve.wait_ge(s_rtw, 32)
                dve.tensor_tensor(logits[:, c, :], bank(4 + c % 2)[:, 0:E], bias[:, :], ALU.add).then_inc(s_lgc, 1)

            def over_e(x, tiles=NT):
                return x.unsqueeze(2).to_broadcast([P, tiles, E])

            def half_tiles(q):
                return slice(q * (NT // 2), (q + 1) * (NT // 2))

            def router_shift(q):
                r = half_tiles(q)
                dve.wait_ge(s_lgc, (q + 1) * (NT // 2))
                step(dve.tensor_reduce(row_red[:, r], logits[:, r, :], AX.X, ALU.max))
                dve.tensor_tensor(logits[:, r, :], logits[:, r, :], over_e(row_red[:, r], NT // 2),
                                  ALU.subtract).then_inc(s_shift, 1)

            def router_probs(q):
                r = half_tiles(q)
                dve.wait_ge(s_exp, q + 1)
                step(dve.tensor_reduce(row_red[:, r], probs_e[:, r, :], AX.X, ALU.add))
                step(dve.reciprocal(row_red[:, r], row_red[:, r]))
                step(dve.tensor_tensor(probs_e[:, r, :], probs_e[:, r, :], over_e(row_red[:, r], NT // 2), ALU.mult))

            def top2(c0, c1):
                for c in range(c0, c1):
                    step(dve.max(top_v[:, c, :], probs_e[:, c, :]))
                    step(dve.max_index(top_i[:, c, :], top_v[:, c, :], probs_e[:, c, :]))

            def attention_low(c):
                dve.wait_ge(s_athi, c + 1)
                if c == 0:
                    dve.wait_ge(s_AT, ATT_DONE)
                if c >= 2:
                    dve.wait_ge(s_op, c - 1)
                four = [x[:, c % 2, :].rearrange("p (g n) -> p g n", g=GROUPS) for x in (at_lo, at_hi)]
                dve.tensor_tensor(four[0], attn_tile(c), four[1].bitcast(F32), ALU.subtract).then_inc(s_atlo, 1)

            attention_low(0)
            for c in range(NT + 3):
                if c + 1 < NT:
                    attention_low(c + 1)
                if c < NT:
                    residual(c)
                if 1 <= c <= NT:
                    norm2(c - 1)
                if c >= 3:
                    logit(c - 3)
                if c == NT // 2 + 2:
                    router_shift(0)
                if c == NT // 2 + 3:
                    router_probs(0)
                if NT // 2 + 4 <= c < NT:
                    top2(2 * (c - NT // 2 - 4), 2 * (c - NT // 2 - 4) + 2)

            def weights():
                step(dve.tensor_tensor(w_sum[:, :], top_v[:, :, 0], top_v[:, :, 1], ALU.add))
                step(dve.tensor_scalar(w_sum[:, :], w_sum[:, :], W_EPS, None, ALU.add))
                step(dve.reciprocal(w_sum[:, :], w_sum[:, :]))
                step(dve.tensor_tensor(w_top[:, :, :], top_v[:, :, 0:TOPK],
                                       w_sum[:, :].unsqueeze(2).to_broadcast([P, NT, TOPK]), ALU.mult))
                step(dve.tensor_copy(top_f[:, :, :], top_i[:, :, 0:TOPK]))
                for k in range(TOPK):
                    step(dve.tensor_tensor(oh_e[:, k, :, :], iota_e[:, :].unsqueeze(1).to_broadcast([P, NT, E]),
                                           over_e(top_f[:, :, k]), ALU.is_equal))
                dve.tensor_tensor(oh_any[:, :, :], oh_e[:, 0, :, :], oh_e[:, 1, :, :], ALU.add).then_inc(s_oh, 1)

            def places():
                dve.wait_ge(s_rank, 1)
                step(dve.tensor_copy(count_e[:, :], bank(0)[:, NT * E:NT * E + E]))
                ee = [P, E, E]
                step(dve.tensor_tensor(cmp_e[:, :, :], count_e[:, :].unsqueeze(2).to_broadcast(ee),
                                       iota_p128[:, :].unsqueeze(1).to_broadcast(ee), ALU.is_gt))
                step(dve.tensor_reduce(tiles_e[:, :], cmp_e[:, :, :], AX.X, ALU.add))
                step(dve.tensor_scalar(tiles_e[:, :], tiles_e[:, :], 1.0, None, ALU.max))
                step(dve.tensor_tensor(cmp_e[:, :, :], tiles_e[:, :].unsqueeze(1).to_broadcast(ee),
                                       upto_e[:, :, :], ALU.mult))
                step(dve.tensor_reduce(tiles_to[:, :], cmp_e[:, :, :], AX.X, ALU.add))
                step(dve.tensor_tensor(base_e[:, :], tiles_to[:, :], tiles_e[:, :], ALU.subtract))
                step(dve.tensor_scalar(base_e[:, :], base_e[:, :], float(P), None, ALU.mult))
                dve.tensor_copy(tiles_to_i[:, :], tiles_to[:, :]).then_inc(s_plan, 1)

            def choice_places():
                rank = bank(0)[:, 0:NT * E].rearrange("p (c e) -> p c e", e=E)
                step(dve.tensor_tensor(pos_all[:, :, :], rank, base_e[:, :].unsqueeze(1).to_broadcast([P, NT, E]),
                                       ALU.add))
                for k in range(TOPK):
                    step(dve.tensor_tensor(pos_pick[:, :, :], oh_e[:, k, :, :], pos_all[:, :, :], ALU.mult))
                    step(dve.tensor_reduce(pos_f[:, k, :], pos_pick[:, :, :], AX.X, ALU.add))
                step(dve.tensor_copy(pos_i[:, :, :], pos_f[:, :, :]))
                step(dve.tensor_scalar(pos_hl[:, 0, :, :], pos_i[:, :, :], 7, None, ALU.arith_shift_right))
                step(dve.tensor_scalar(pos_hl[:, 1, :, :], pos_i[:, :, :], P - 1, None, ALU.bitwise_and))
                step(dve.tensor_copy(pos_hlf[:, :, :, :], pos_hl[:, :, :, :]))

            def tile_experts():
                je = [P, TILES, E]
                step(dve.tensor_tensor(cmp_j[:, :, :], tiles_to[:, :].unsqueeze(1).to_broadcast(je),
                                       iota_j[:, :].unsqueeze(2).to_broadcast(je), ALU.is_le))
                step(dve.tensor_reduce(tile_e[:, :], cmp_j[:, :, :], AX.X, ALU.add))
                dve.tensor_scalar(tile_e_i[:, :], tile_e[:, :], float(E - 1), None, ALU.min).then_inc(s_plan, 1)

            def slot_onehots(n0, n1):
                for n in range(n0, n1):
                    c, k, r = n // TOPK, n % TOPK, n % SLOT_RING
                    if n >= SLOT_RING:
                        dve.wait_ge(s_slotm, n - SLOT_RING + 1)
                    dve.tensor_scalar(slot_lo[:, r, :], iota_f[:, :], pos_hlf[:, 1, k, c:c + 1], None,
                                      ALU.is_equal).then_inc(s_slot, 1)
                    dve.tensor_scalar(slot_hi[:, r, 0, :], iota_j[:, :], pos_hlf[:, 0, k, c:c + 1],
                                      tok_no1[:, c:c + 1], ALU.is_equal, ALU.mult).then_inc(s_slot, 1)
                    dve.tensor_scalar(slot_hi[:, r, 1, :], iota_j[:, :], pos_hlf[:, 0, k, c:c + 1],
                                      w_top[:, c, k:k + 1], ALU.is_equal, ALU.mult).then_inc(s_slot, 1)

            def slot_tokens():
                dve.wait_ge(s_slotm, TOPK * NT)
                dve.tensor_copy(slot_w[:, :], bank(1)[:, TILES:2 * TILES]).then_inc(s_plan, 1)
                step(dve.tensor_scalar(slot_f[:, :], bank(1)[:, 0:TILES], -1.0, None, ALU.add))
                dve.tensor_scalar(slot_tok[:, :], slot_f[:, :], 0.0, None, ALU.max).then_inc(s_plan, 1)
                step(dve.tensor_scalar(pad_row[:, :], tok_no1[:, 0:1], float(T), None, ALU.add))
                step(dve.tensor_scalar(slot_pad[:, :], slot_f[:, :], 0.0, pad_row[:, :], ALU.is_lt, ALU.mult))
                dve.tensor_tensor(slot_out[:, :], slot_pad[:, :], slot_f[:, :], ALU.add).then_inc(s_plan, 1)

            def gate(n, p):
                dve.wait_ge(s_silu, n + 1)
                if not isinstance(n, int) or n >= 2:
                    dve.wait_ge(s_gT, n - 1)
                dve.tensor_tensor(gated[:, p, :], silu_g[:, p, :], bank(2 + p)[:, FF:2 * FF],
                                  ALU.mult).then_inc(s_gated, 1)

            def turn_low(n):
                dve.wait_ge(s_gshi, n + 1)
                dve.tensor_tensor(gs_lo[:, n % 2, :], bank(4 + n % 2)[:, 0:FF], gs_hi[:, n % 2, :].bitcast(F32),
                                  ALU.subtract).then_inc(s_gC, 1)

            def shared_add(c):
                dve.wait_ge(s_y, c + 1)
                dve.tensor_tensor(acc[:, c, :], acc[:, c, :], bank(6 + c % 2), ALU.add).then_inc(s_acc, 1)

            router_shift(1)
            dve.wait_ge(s_moec, 7)
            for n in range(SHARED):
                if n >= 1:
                    turn_low(n - 1)
                gate(n, n % 2)
                if n >= 2:
                    shared_add(n - 2)
                if n == 0:
                    router_probs(1)
                    top2(NT // 2, NT // 2 + 3)
                if n == 1:
                    top2(NT // 2 + 3, NT)
                if n == 2:
                    weights()
                if n == 4:
                    places()
                if n == 5:
                    choice_places()
                if n == SLOT0 + 7:
                    tile_experts()
                if SLOT0 <= n < SLOT0 + 7:
                    slot_onehots(5 * (n - SLOT0), min(5 * (n - SLOT0) + 5, TOPK * NT))
                if n == SLOT0 + 8:
                    slot_tokens()

            def row_copy(m, s, first):
                dve.wait_ge(s_xT2, 2 * m + (s + 1))
                if not first:
                    dve.wait_ge(s_gu, SHARED + 2 * m + (s - 1))
                dve.tensor_copy(x_T[:, s, :], bank(s)).then_inc(s_xC2, 1)

            shared_add(SHARED - 2)
            row_copy(0, 0, True)
            turn_low(SHARED - 1)
            row_copy(0, 1, True)
            shared_add(SHARED - 1)
            gate(SHARED, 0)
            with dve.Fori(1, TILES // 2) as m:
                row_copy(m, 0, False)
                gate(SHARED + 2 * m - 1, 1)
                row_copy(m, 1, False)
                gate(SHARED + 2 * m, 0)
            row_copy(TILES // 2, 0, False)
            gate(SHARED + LAST - 1, 1)
            gate(SHARED + LAST, 0)

        def moe_pe(pe):
            def shared_gate_up(n, k0, k1):
                p = n % 2
                if k0 == 0:
                    pe.wait_ge(s_xslo, n + 1)
                    if n >= 2:
                        pe.wait_ge(s_gated, n - 1)
                for k in range(k0, k1):
                    for t, (x, w) in enumerate(((xs_hi, ws_hi), (xs_lo, ws_hi), (xs_hi, ws_lo))):
                        mm = pe.matmul(bank(2 + p), x[:, p, k * P:(k + 1) * P], w[:, k, :],
                                       start=(k == 0 and t == 0), stop=(k == KC - 1 and t == 2),
                                       skip_group_check=True)
                if k1 == KC:
                    mm.then_inc(s_gu, 1)

            pe.wait_ge(s_AT, ATT_DONE)
            pe.wait_ge(s_wolo, KC)
            for c in range(NT + 3):
                if c < NT:
                    if c >= 2:
                        pe.wait_ge(s_var2, c - 1)
                    pe.wait_ge(s_atlo, c + 1)
                    for g in range(GROUPS):
                        for t, (x, w) in enumerate(((at_hi, wo_hi), (at_lo, wo_hi), (at_hi, wo_lo))):
                            mm = pe.matmul(bank(c % 2), x[:, c % 2, g * P:(g + 1) * P], w[:, g, :],
                                           start=(g == 0 and t == 0), stop=(g == GROUPS - 1 and t == 2))
                    mm.then_inc(s_op, 1)
                if 2 <= c <= NT + 1:
                    t = c - 2
                    pe.wait_ge(s_xn2, t + 1)
                    if t >= 2:
                        pe.wait_ge(s_x2C, t - 1)
                    for k in range(KC):
                        mm = pe.transpose(bank(2 + t % 2)[:, k * P:(k + 1) * P], xn2[:, t % 2, k * P:(k + 1) * P],
                                          ident[:, :])
                    mm.then_inc(s_x2T, 1)
                if c == NT + 1:
                    pe.wait_ge(s_wslo, NT)
                    pe.wait_ge(s_x2C, NT - 1)
                    shared_gate_up(0, 0, KC)
                if c >= 3:
                    t = c - 3
                    if t == 0:
                        pe.wait_ge(s_rtw, 32)
                    pe.wait_ge(s_x2C, t + 1)
                    if t >= 2:
                        pe.wait_ge(s_lgc, t - 1)
                    for k in range(KC):
                        mm = pe.matmul(bank(4 + t % 2)[:, 0:E], xnT[:, k, t * P:(t + 1) * P], wr[:, k, :],
                                       start=(k == 0), stop=(k == KC - 1))
                    mm.then_inc(s_lg, 1)

            def ranks():
                pe.wait_ge(s_oh, 1)
                b = bank(0)
                flat = oh_any[:, :, :].rearrange("p c e -> p (c e)")
                pe.matmul(b[:, 0:NT * E], tri_bf[:, :], flat, start=True, stop=False, skip_group_check=True)
                for c in range(NT):
                    if c < NT - 1:
                        pe.matmul(b[:, (c + 1) * E:NT * E].rearrange("p (c e) -> p c e", e=E), ones_bf[:, :],
                                  oh_any[:, c, :].unsqueeze(1).to_broadcast([P, NT - 1 - c, E]),
                                  start=False, stop=False, skip_group_check=True)
                    mm = pe.matmul(b[:, NT * E:NT * E + E], ones_bf[:, :], oh_any[:, c, :], start=False,
                                   stop=(c == NT - 1), skip_group_check=True)
                mm.then_inc(s_rank, 1)

            def slots(n0, n1):
                for n in range(n0, n1):
                    pe.wait_ge(s_slot, 3 * n + 3)
                    pe.matmul(bank(1)[:, 0:2 * TILES], slot_lo[:, n % SLOT_RING, :],
                              slot_hi[:, n % SLOT_RING, :, :].rearrange("p a n -> p (a n)"), start=(n == 0),
                              stop=(n == TOPK * NT - 1), skip_group_check=True).then_inc(s_slotm, 1)

            def gate_up(n, p, k0, k1, ring):
                if k0 == 0:
                    pe.wait_ge(s_gated, n - 1)
                for k in range(k0, k1):
                    mm = pe.matmul(bank(2 + p), x_T[:, p, k * P:(k + 1) * P],
                                   w_gu[:, bass.ds(ring, 1), k, :].rearrange("p o n -> p (o n)"),
                                   start=(k == 0), stop=(k == KC - 1), skip_group_check=True)
                if k1 == KC:
                    mm.then_inc(s_gu, 1)

            def turn_gated(n, p):
                pe.wait_ge(s_gated, n + 1)
                if not isinstance(n, int) or n >= 2:
                    pe.wait_ge(s_gC, n - 1)
                for k in range(2):
                    mm = pe.transpose(bank(4 + p)[:, k * P:(k + 1) * P], gated[:, p, k * P:(k + 1) * P], ident[:, :])
                mm.then_inc(s_gT, 1)

            def shared_down(n):
                p = n % 2
                pe.wait_ge(s_gC, n + 1)
                if n >= 2:
                    pe.wait_ge(s_acc, n - 1)
                for k in range(2):
                    for t, (g, w) in enumerate(((gs_hi, ws_hi), (gs_lo, ws_hi), (gs_hi, ws_lo))):
                        mm = pe.matmul(bank(6 + p), g[:, p, k * P:(k + 1) * P], w[:, KC + k, :],
                                       start=(k == 0 and t == 0), stop=(k == 1 and t == 2))
                mm.then_inc(s_y, 1)

            for n in range(SHARED):
                if n:
                    shared_gate_up(n, 0, 2)
                    turn_gated(n - 1, (n - 1) % 2)
                    shared_gate_up(n, 2, KC)
                if n >= 1:
                    shared_down(n - 1)
                if n == 3:
                    ranks()
                if SLOT0 < n <= SLOT0 + 7:
                    slots(5 * (n - SLOT0 - 1), min(5 * (n - SLOT0 - 1) + 5, TOPK * NT))

            def turn_rows(m, s, first):
                pe.wait_ge(s_xg[s], 16 * (m + 1))
                if not first:
                    pe.wait_ge(s_xC2, 2 * m + (s - 1))
                for k in range(KC):
                    mm = pe.transpose(bank(s)[:, k * P:(k + 1) * P], x_rows[s][:, k * P:(k + 1) * P], ident[:, :])
                mm.then_inc(s_xT2, 1)

            def routed(m, s, before, after):
                n = SHARED + 2 * m + s
                e = pe.value_load(tile_e_i[0:1, bass.ds(2 * m + s, 1)], min_val=0, max_val=E - 1)
                ring = pe.snap(e % WRING)
                ring_before = ring_slot(2 * m + (s - 1)) if before else None
                pe.wait_ge(s_wr, e + 1)
                pe.wait_ge(s_xC2, 2 * m + (s + 1))
                gate_up(n, s, 0, 2, ring)
                turn_gated(n - 1, 1 - s)
                gate_up(n, s, 2, KC, ring)
                if after is not None:
                    turn_rows(*after)
                if before:
                    down_of(n - 1, 1 - s, 2 * m + (s - 1), ring_before)
                else:
                    shared_down(SHARED - 1)

            def ring_slot(j):
                e = pe.value_load(tile_e_i[0:1, bass.ds(j, 1)], min_val=0, max_val=E - 1)
                return pe.snap(e % WRING)

            def down_of(n, p, j, ring):
                pe.wait_ge(s_gC, n + 1)
                if isinstance(j, int) and j < 2:
                    pe.wait_ge(s_acc, SHARED + j - 1)
                else:
                    pe.wait_ge(s_yc, j - 1)
                for k in range(2):
                    mm = pe.matmul(bank(6 + p), gated_T[:, p, k * P:(k + 1) * P],
                                   w_dn[:, bass.ds(ring, 1), k, :].rearrange("p o n -> p (o n)"), start=(k == 0),
                                   stop=(k == 1))
                mm.then_inc(s_y, 1)

            pe.wait_ge(s_plan, PLANNED)
            turn_rows(0, 0, True)
            routed(0, 0, False, (0, 1, True))
            routed(0, 1, True, (1, 0, False))
            routed(1, 0, True, (1, 1, False))
            with pe.Fori(2, TILES // 2) as m:
                routed(m - 1, 1, True, (m, 0, False))
                routed(m, 0, True, (m, 1, False))
            routed(TILES // 2 - 1, 1, True, (TILES // 2, 0, False))
            routed(TILES // 2, 0, True, None)
            turn_gated(SHARED + LAST, 0)
            down_of(SHARED + LAST, 0, LAST, ring_slot(LAST))

        @block.sync
        def _(sp):
            sp.dma_start(hot_ids[:, :], a["hot_ids"]).then_inc(s_in, 16)
            sp.dma_start(tok_ids[:, :], a["tok_ids"]).then_inc(s_in, 16)
            sp.dma_start(projT[:, :], a["projT"]).then_inc(s_proj, 16)
            sp.wait_ge(s_table, 1)
            load_w(sp, 0)
            for c in range(NT):
                sp.wait_ge(s_h, c + 1)
                sp.dma_start(h_dram[c * P:(c + 1) * P, :], hot_vec[c][:, :]).then_inc(s_hst, 16)
                if c == NT - LAG:
                    stack(sp, 0, 0, (0,), first=True)
            stack(sp, 0, 0, (1,), first=True)
            att_sp(sp)
            moe_sp(sp)

        @block.gpsimd
        def _(pool):
            for s in (s_lo, s_hi):
                pool.sem_inc(s, HEAD)
            for m, v in ((ident, 0.0), (ident_bf, 0.0), (tri_bf, 1.0), (mask_bf, 0.0)):
                pool.memset(m[:, :], v).then_inc(s_pool, 1)
            pool.memset(ones_bf[:, :], 1.0).then_inc(s_const, 1)
            pool.memset(half_neg[:, :], -0.5).then_inc(s_const, 1)
            pool.iota(iota_bf[:, :], pattern=[[1, 256]], base=0, channel_multiplier=0,
                      allow_small_or_imprecise_dtypes=True).then_inc(s_const, 1)
            pool.iota(row64[:, :], pattern=[[0, 1]], base=0, channel_multiplier=HOT_C,
                      allow_small_or_imprecise_dtypes=True).then_inc(s_const, 1)
            pool.iota(chunk1[:, :], pattern=[[1, HOT_C]], base=1, channel_multiplier=0,
                      allow_small_or_imprecise_dtypes=True).then_inc(s_const, 1)
            for m, pattern, base, rows in (
                    (iota_e, [[1, E]], 0, 0), (iota_p128, [[P, T // P]], 0, 0), (iota_j, [[1, TILES]], 0, 0),
                    (iota_f, [[1, P]], 0, 0), (tok_no1, [[P, NT]], 1, 1)):
                pool.iota(m[:, :], pattern=pattern, base=base, channel_multiplier=rows,
                          allow_small_or_imprecise_dtypes=True).then_inc(s_moec, 1)
            pool.memset(upto_e[:, :, :], 1.0).then_inc(s_moec, 1)
            pool.wait_ge(s_moec, 6)
            pool.affine_select(out=upto_e[:, :, :], in_=upto_e[:, :, :], compare_op=ALU.is_ge, fill=0.0, base=0,
                               pattern=[[1, E], [-1, E]], channel_multiplier=0).then_inc(s_moec, 1)
            pool.wait_ge(s_pool, 4)
            for m in (ident, ident_bf):
                pool.affine_select(out=m[:, :], in_=m[:, :], compare_op=ALU.not_equal, fill=1.0, base=0,
                                   pattern=[[-1, P]], channel_multiplier=1).then_inc(s_const, 1)
            pool.affine_select(out=tri_bf[:, :], in_=tri_bf[:, :], compare_op=ALU.is_gt, fill=0.0, base=0,
                               pattern=[[1, P]], channel_multiplier=-1).then_inc(s_const, 1)
            pool.affine_select(out=mask_bf[:, :], in_=mask_bf[:, :], compare_op=ALU.is_ge, fill=1e9, base=0,
                               pattern=[[-1, P]], channel_multiplier=1).then_inc(s_const, 1)
            for c in range(NT):
                pool.memset(hot_vec[c][:, :], 0.0).then_inc(s_zero, 1)
                pool.memset(cold_lat[c][:, :], 0.0).then_inc(s_zero, 1)
            pool.wait_ge(s_zero, 2 * NT)
            for c in range(NT):
                pool.wait_ge(s_rows, c // PER + 1)
                pool.indirect_dma_start(
                    out=cold_lat[c][:, :], out_offset=None, in_=a["cold_emb"],
                    in_offset=bass.IndirectOffsetOnAxis(ap=cold_row[:, c:c + 1], axis=0),
                    bounds_check=NUM_COLD - 1, oob_is_err=False).then_inc(s_coldg[c], 16)
                pool.indirect_dma_start(
                    out=hot_vec[c][:, :], out_offset=None, in_=a["hot_emb"],
                    in_offset=bass.IndirectOffsetOnAxis(ap=hot_row[:, c:c + 1], axis=0),
                    bounds_check=NUM_HOT - 1, oob_is_err=False).then_inc(s_hotg[c], 16)
                if c >= LAG + 1:
                    inv_std(pool, c - LAG - 1)
            for c in range(NT - LAG - 1, NT):
                inv_std(pool, c)
                if c < NT - 1:
                    half = c - NT + LAG + 1
                    split_part(pool, 0, 0, half // 2, half % 2, None)
            att_pool(pool)
            moe_pool(pool)

        @block.scalar
        def _(act):
            for s in (s_E, s_Ca, s_fact, s_ZR):
                act.sem_inc(s, HEAD)
            act.wait_ge(s_const, 9)
            for c in range(HOT_C):
                act.wait_ge(s_ohhi, c + 1)
                act.activation(oh_hi_row[:, c, :], oh_hi[:, c, :], ACT.Copy, scale=row64[:, :]).then_inc(s_row, 1)
                if c % 2:
                    act.wait_ge(s_ohlo, c + 1)
                    act.activation(oh_lo[:, c, 1, :], oh_lo[:, c, 0, :], ACT.Copy,
                                   scale=chunk1[:, c:c + 1]).then_inc(s_chunk_act, 1)
            for k in range(2):
                act.wait_ge(s_tohT, k + 1)
                act.copy(tok_ohT[:, 8 * k:8 * k + 8, :].rearrange("p a n -> p (a n)"),
                         bank(2 + k).bitcast(BF16)[0:HI, :]).then_inc(s_tohC, 1)
            for c in range(NT + 3):
                if c < NT:
                    act.wait_ge(s_coldT, c + 1)
                    if c >= 2:
                        act.wait_ge(s_cvec, c - 1)
                    act.copy(cold_T[:, c % 2, :], bank(6 if c % 2 else 0)[:, 0:P]).then_inc(s_coldC, 1)
                if c >= 3:
                    t = c - 3
                    act.wait_ge(s_xT, t + 1)
                    act.copy(xnT[:, :, t * P:(t + 1) * P],
                             bank(2 + t % 2).rearrange("p (k n) -> p k n", k=KC)).then_inc(s_xC, 1)
                if 0 <= c - FILL0 < FILLS:
                    fill_evac(act, "act", 0, c - FILL0, 0)
            att_act(act)
            moe_act(act)

        @block.vector
        def _(dve):
            for s in (s_M, s_Cd, s_Zr, s_Z, s_AT, s_fdve):
                dve.sem_inc(s, HEAD)
            step = Chain(dve, s_dve)
            dve.wait_ge(s_in, 32)
            dve.wait_ge(s_const, 9)

            def split_ids(raw, f, wrap, ints, hi, lo, clamp):
                step(dve.tensor_copy(f[:, :], raw[:, :]))
                step(dve.tensor_scalar(wrap[:, :], f[:, :], 0.0, float(VOCAB), ALU.is_lt, ALU.mult))
                step(dve.tensor_tensor(f[:, :], f[:, :], wrap[:, :], ALU.add))
                if clamp:
                    step(dve.tensor_scalar(f[:, :], f[:, :], 0.0, float(VOCAB - 1), ALU.max, ALU.min))
                step(dve.tensor_copy(ints[:, 0, :], f[:, :]))
                step(dve.tensor_scalar(ints[:, 1, :], ints[:, 0, :], 255, None, ALU.bitwise_and))
                step(dve.tensor_copy(lo[:, :], ints[:, 1, :]))
                step(dve.tensor_scalar(ints[:, 0, :], ints[:, 0, :], 8, None, ALU.arith_shift_right))
                step(dve.tensor_copy(hi[:, :], ints[:, 0, :]))

            split_ids(hot_ids, hot_f, hot_wrap, hot_i, hot_hi, hot_lo, False)
            for c in range(HOT_C):
                dve.tensor_scalar(oh_hi[:, c, :], iota_bf[0:HOT_P, 0:HI], hot_hi[:, c:c + 1], None,
                                  ALU.is_equal).then_inc(s_ohhi, 1)
                dve.tensor_scalar(oh_lo[:, c, 0, :], iota_bf[0:HOT_P, :], hot_lo[:, c:c + 1], None,
                                  ALU.is_equal).then_inc(s_ohlo, 1)
                if c % 2 == 0:
                    dve.tensor_scalar(oh_lo[:, c, 1, :], iota_bf[0:HOT_P, :], hot_lo[:, c:c + 1],
                                      chunk1[:, c:c + 1], ALU.is_equal, ALU.mult).then_inc(s_chunk, 1)
            split_ids(tok_ids, tok_f, tok_wrap, tok_i, tok_hi, tok_lo, True)
            for c in range(NT):
                dve.tensor_scalar(tok_oh[:, c, :], iota_bf[:, 0:HI], tok_hi[:, c:c + 1], None,
                                  ALU.is_equal).then_inc(s_toh, 1)
            dve.wait_ge(s_table, 1)
            tb = bank(0)
            step(dve.tensor_scalar(seen[:, :], tb[0:HI, 0:256], 1.0, None, ALU.min))
            step(dve.tensor_reduce(seen_n[:, :], seen[:, :], AX.X, ALU.add))
            dve.tensor_copy(seen_b[:, :], seen_n[:, :]).then_inc(s_seen, 1)
            step(dve.tensor_scalar(rank_i[:, 0, :], tb[0:HI, 256:512], float(NUM_HOT), None, ALU.min))
            step(dve.tensor_scalar(rank_i[:, 1, :], rank_i[:, 0, :], ~127, None, ALU.bitwise_and))
            step(dve.tensor_copy(tab_a[:, 256:512], rank_i[:, 1, :]))
            step(dve.tensor_scalar(rank_i[:, 1, :], rank_i[:, 0, :], 127, None, ALU.bitwise_and))
            step(dve.tensor_copy(tab_b[:, :], rank_i[:, 1, :]))
            dve.wait_ge(s_base, 1)
            step(dve.tensor_copy(rank_i[:, 0, 0:1], bank(1)[0:HI, 0:1]))
            step(dve.tensor_scalar(rank_i[:, 1, 0:1], rank_i[:, 0, 0:1], 127, None, ALU.bitwise_and))
            step(dve.tensor_scalar(rank_i[:, 2, 0:1], rank_i[:, 0, 0:1], ~127, None, ALU.bitwise_and))
            step(dve.tensor_copy(tab_c[:, :], rank_i[:, 2, 0:1]))
            step(dve.tensor_tensor(seen[:, 0:1], seen[:, 0:1], rank_i[:, 1, 0:1], ALU.add))
            dve.tensor_copy(tab_a[:, 0:256], seen[:, :]).then_inc(s_tab, 1)

            def look_up(c):
                s = c % 2
                if c >= 2:
                    dve.wait_ge(s_looked, 2 * (c - 1))
                dve.wait_ge(s_look, c + 1)
                for part, test, total in ((0, ALU.is_le, below), (1, ALU.is_equal, hot_no)):
                    dve.scalar_tensor_tensor(out=prod[:, s, part, :], in0=iota_bf[:, :], scalar=tok_lo[:, c:c + 1],
                                             in1=bank(4 + s)[:, 256 * part:256 * part + 256], op0=test,
                                             op1=ALU.mult, accum_out=total[:, c:c + 1]).then_inc(s_looked, 1)

            def row_numbers(k):
                r = slice(k * PER, (k + 1) * PER)
                dve.wait_ge(s_looked, 2 * (k + 1) * PER)
                step(dve.tensor_scalar(tmp_a[:, r], hot_no[:, r], 0.0, SKIP, ALU.is_equal, ALU.mult))
                step(dve.tensor_tensor(tmp_a[:, r], tmp_a[:, r], hot_no[:, r], ALU.add))
                dve.tensor_scalar(hot_row[:, r], tmp_a[:, r], -1.0, None, ALU.add).then_inc(s_dve, 1)
                step.n += 1
                step(dve.tensor_tensor(tmp_b[:, r], tok_f[:, r], below[:, r], ALU.subtract))
                step(dve.tensor_scalar(tmp_b[:, r], tmp_b[:, r], 0.0, float(NUM_COLD - 1), ALU.max, ALU.min))
                step(dve.tensor_scalar(tmp_a[:, r], hot_no[:, r], 0.0, SKIP, ALU.is_gt, ALU.mult))
                dve.tensor_tensor(cold_row[:, r], tmp_a[:, r], tmp_b[:, r], ALU.add).then_inc(s_rows, 1)

            def embed(c):
                s = c % 2
                dve.wait_ge(s_cvec, c + 1)
                dve.wait_ge(s_hotg[c], 16)
                hv = hot_vec[c]
                dve.tensor_tensor(hv[:, :], hv[:, :], bank(5 if s else 1), ALU.add).then_inc(s_h, 1)
                dve.wait_ge(s_h, c + 1)
                step(dve.bn_stats(stats[:, s, :], hv[:, :]))
                step(dve.bn_aggr(mv[:, s, :], stats[:, s, :]))
                dve.tensor_scalar(mv[:, s, 1:2], mv[:, s, 1:2], LN_EPS, None, ALU.add).then_inc(s_var, 1)

            def norm(c):
                s = c % 2
                dve.wait_ge(s_rstd, c + 1)
                if c >= 2:
                    dve.wait_ge(s_xT, c - 1)
                dve.tensor_scalar(xn[:, s, :], hot_vec[c][:, :], mv[:, s, 0:1], rstd[:, s:s + 1],
                                  ALU.subtract, ALU.mult).then_inc(s_xn, 1)

            for k in range(BATCHES):
                for c in range(k * PER, (k + 1) * PER):
                    look_up(c)
                row_numbers(k)
            for c in range(NT + 1):
                if c < NT:
                    embed(c)
                if c >= 1:
                    norm(c - 1)
                if 0 <= c + 1 - FILL0 < FILLS:
                    fill_evac(dve, "dve", 0, c + 1 - FILL0, 0)
            att_dve(dve)
            moe_dve(dve)

        @block.tensor
        def _(pe):
            for s in (s_S, s_T, s_fill, s_PV):
                pe.sem_inc(s, HEAD)
            pe.wait_ge(s_const, 9)
            for c in range(HOT_C):
                pe.wait_ge(s_ohlo, c + 1)
                pe.wait_ge(s_chunk_act if c % 2 else s_chunk, c // 2 + 1)
                pe.wait_ge(s_row, c + 1)
                pe.matmul(bank(0)[0:HI, :], oh_hi[:, c, :], oh_lo[:, c, :, :].rearrange("p a n -> p (a n)"),
                          start=(c == 0), stop=False, skip_group_check=True)
                mm = pe.matmul(bank(0)[0:HI, 256:512], oh_hi_row[:, c, :], oh_lo[:, c, 0, :],
                               start=False, stop=(c == HOT_C - 1), skip_group_check=True)
            mm.then_inc(s_table, 1)
            for k in range(2):
                pe.wait_ge(s_toh, 8 * k + 8)
                for c in range(8):
                    mm = pe.transpose(bank(2 + k).bitcast(BF16)[0:HI, c * P:(c + 1) * P], tok_oh[:, 8 * k + c, :],
                                      ident_bf[:, :])
                mm.then_inc(s_tohT, 1)
            pe.wait_ge(s_seen, 1)
            pe.matmul(bank(1)[0:HI, 0:1], tri_bf[0:HI, 0:HI], seen_b[:, :], start=True,
                      stop=True).then_inc(s_base, 1)
            pe.wait_ge(s_tab, 1)
            pe.wait_ge(s_tohC, 2)
            for c in range(NT):
                if c >= 2:
                    pe.wait_ge(s_looked, 2 * (c - 1))
                b = bank(4 + c % 2)
                oh = tok_ohT[:, c, :]
                pe.matmul(b, oh, tab_a[:, :], start=True, stop=False, skip_group_check=True)
                pe.matmul(b[:, 256:512], oh, tab_b[:, :], start=False, stop=False, skip_group_check=True)
                pe.matmul(b[:, 0:1], oh, tab_c[:, :], start=False, stop=True,
                          skip_group_check=True).then_inc(s_look, 1)
            pe.wait_ge(s_proj, 16)
            for c in range(NT + 3):
                if c < NT:
                    pe.wait_ge(s_coldg[c], 16)
                    if c >= 2:
                        pe.wait_ge(s_coldC, c - 1)
                    pe.transpose(bank(6 if c % 2 else 0)[:, 0:P], cold_lat[c][:, :],
                                 ident[:, :]).then_inc(s_coldT, 1)
                if 1 <= c <= NT:
                    t = c - 1
                    pe.wait_ge(s_coldC, t + 1)
                    if t == 1:
                        pe.wait_ge(s_looked, 2 * NT)
                    if t >= 2:
                        pe.wait_ge(s_h, t - 1)
                    pe.matmul(bank(5 if t % 2 else 1), cold_T[:, t % 2, :], projT[:, :], start=True,
                              stop=True).then_inc(s_cvec, 1)
                if c >= 3:
                    t = c - 3
                    pe.wait_ge(s_xn, t + 1)
                    if t >= 2:
                        pe.wait_ge(s_xC, t - 1)
                    for k in range(KC):
                        mm = pe.transpose(bank(2 + t % 2)[:, k * P:(k + 1) * P], xn[:, t % 2, k * P:(k + 1) * P],
                                          ident[:, :])
                    mm.then_inc(s_xT, 1)
                if 0 <= c - FILL0 < FILLS:
                    pe.wait_ge(s_xC, NT // BATCH)
                    for k in range(KC):
                        fill_piece(pe, 0, 0, c - FILL0, k, 16)
            pe.wait_ge(s_xC, NT)
            att_pe(pe)
            moe_pe(pe)


def layouts(f):
    import numpy as np

    c = np.ascontiguousarray

    def gate_up(wg, wu):
        return c(np.concatenate([wg, wu], -1).reshape(-1, KC, P, D).transpose(0, 2, 1, 3))

    def down(wd):
        return c(wd.reshape(-1, FF // P, P, D).transpose(0, 2, 1, 3))

    return {
        "tok_ids": c(f["x"].reshape(NT, P).T),
        "hot_ids": c(f["L0_tok_hot_token_ids"].reshape(HOT_P, HOT_C)),
        "hot_emb": c(f["L0_tok_hot_emb_w"]),
        "cold_emb": c(f["L0_tok_cold_emb_w"]),
        "projT": c(f["L0_tok_proj_w"].T),
        "wqkv": c(f["L0_attn_w_project"].reshape(3, GROUPS, P, KC, P).transpose(1, 4, 3, 0, 2)
                  .reshape(GROUPS, P, KC, 3 * P)),
        "woT": c(f["L0_attn_w_out"].T.reshape(KC, P, D).transpose(1, 0, 2)),
        "wrT": c(f["L0_ffn_Wr"].T.reshape(KC, P, E).transpose(1, 0, 2)),
        "bias": c(np.broadcast_to(f["L0_ffn_bias"], (P, E))),
        "wgu": gate_up(f["L0_ffn_Wg"], f["L0_ffn_Wu"]),
        "wd": down(f["L0_ffn_Wd"]),
        "sgu": gate_up(f["L0_ffn_sWg"], f["L0_ffn_sWu"])[0],
        "sd": down(f["L0_ffn_sWd"])[0],
    }


def kernel(**inputs):
    import numpy as np
    import concourse.bacc as bacc
    from concourse.bass_utils import run_bass_kernel_spmd

    nc = bacc.Bacc("TRN2", target_bir_lowering=False, num_devices=1)
    arrays, aps = {}, {}
    for name, x in layouts({k: np.asarray(v) for k, v in inputs.items()}).items():
        arrays[f"in_{name}"] = x
        aps[name] = nc.dram_tensor(f"in_{name}", x.shape, mybir.dt.from_np(x.dtype), kind="ExternalInput").ap()
    out = nc.dram_tensor("out_0", (T + P, D), F32, kind="ExternalOutput").ap()
    build(nc, aps, out)
    r = run_bass_kernel_spmd(nc, [arrays], core_ids=[0])
    return r.results[0]["out_0"][:T].reshape(BATCH, SEQ, D)
```
